# Optimizing a Trainium2 kernel written in Bass

```python
import numpy as np
import jax
import jax.numpy as jnp

def _softmax(x, axis=-1):
    return jax.nn.softmax(x, axis=axis)

def _gelu(x):
    return jax.nn.gelu(x, approximate=True)

def _silu(x):
    return jax.nn.silu(x)

def _sigmoid(x):
    return jax.nn.sigmoid(x)

def _layernorm(x, axis=-1, eps=1e-05):
    m = jnp.mean(x, axis=axis, keepdims=True)
    v = jnp.var(x, axis=axis, keepdims=True)
    return (x - m) / jnp.sqrt(v + eps)

def _scatter_add(tgt, idx, src, axis=0):
    return tgt.at[idx].add(src)

def _segment_sum(src, seg, n):
    return jax.ops.segment_sum(src, seg, n)
kernel_name = 'mk_adj_preln_d4_adj_r2_37c2c0'

def setup_inputs(seed: int=0):
    np.random.seed(seed)
    _w = jnp.asarray

    def _rec_inputs():
        import jax
        import jax.numpy as jnp
        _gk = jax.random.key(seed)
        x = -0.0005207 + 1.001 * jax.random.normal(jax.random.fold_in(_gk, 1), (4096, 128), jnp.float32)
        _a = jax.random.bernoulli(jax.random.fold_in(_gk, 2), 0.00195312, (4096, 4096))
        _a = jnp.logical_or(_a, jnp.eye(4096, dtype=bool))
        _af = _a.astype(jnp.float32)
        _af = _af * jax.random.uniform(jax.random.fold_in(_gk, 3), (4096, 4096), jnp.float32, 0.05, 1)
        adj = _af
        return (x, adj)
    x, adj = _rec_inputs()

    def _L0_gnn_setup():
        import jax, jax.numpy as jnp
        import numpy as np
        N = 8192
        C = 128
        F = 128
        key = jax.random.key(seed)
        k1, k2, k3, k4 = jax.random.split(key, 4)
        X = jax.random.normal(k1, (N, C), dtype=jnp.float32)
        adj = jax.random.uniform(k2, (N, N), dtype=jnp.float32)
        W = jax.random.normal(k3, (C, F), dtype=jnp.float32) * 0.05
        b = jax.random.normal(k4, (F,), dtype=jnp.float32) * 0.05
        return {'X': X, 'adj': adj, 'W': W, 'b': b}
    _L0_gnn_all = _L0_gnn_setup()
    _L0_gnn_in = {k: v for k, v in _L0_gnn_all.items() if k in ('W', 'b')}
    del _L0_gnn_all

    def _L1_gnn_setup():
        import jax, jax.numpy as jnp
        import numpy as np
        N, EMB, HID = (4096, 128, 128)
        key = jax.random.key(seed)
        k1, k2, k3, k4, k5, k6, k7, k8 = jax.random.split(key, 8)
        inlayer = jax.random.normal(k1, (N, EMB), dtype=jnp.float32)
        inlayer2 = jax.random.normal(k2, (N, 2 * EMB), dtype=jnp.float32)
        adj_mat = jax.random.randint(k3, (N, N), 0, 2).astype(jnp.float32)
        W1 = jax.random.normal(k4, (HID, 2 * EMB), dtype=jnp.float32) / np.sqrt(2 * EMB)
        w2 = jax.random.normal(k5, (HID,), dtype=jnp.float32) / np.sqrt(HID)
        b2 = jax.random.normal(k6, (), dtype=jnp.float32) * 0.01
        w3 = jax.random.normal(k7, (HID,), dtype=jnp.float32) / np.sqrt(HID)
        b3 = jax.random.normal(k8, (), dtype=jnp.float32) * 0.01
        return {'inlayer': inlayer, 'inlayer2': inlayer2, 'adj_mat': adj_mat, 'W1': W1, 'w2': w2, 'b2': b2, 'w3': w3, 'b3': b3}
    _L1_gnn_all = _L1_gnn_setup()
    _L1_gnn_in = {k: v for k, v in _L1_gnn_all.items() if k in ('inlayer2', 'W1', 'w2', 'b2', 'w3', 'b3')}
    del _L1_gnn_all

    def _L2_gnn_setup():
        import jax, jax.numpy as jnp
        import numpy as np
        N = 4096
        F = 128
        key = jax.random.key(seed)
        k1, k2, k3 = jax.random.split(key, 3)
        x = jax.random.normal(k1, (N, F), dtype=jnp.float32)
        adj = jax.random.uniform(k2, (N, N), dtype=jnp.float32)
        limit = float(np.sqrt(6.0 / (F + F)))
        weight = jax.random.uniform(k3, (F, F), dtype=jnp.float32, minval=-limit, maxval=limit)
        return {'x': x, 'adj': adj, 'weight': weight}
    _L2_gnn_all = _L2_gnn_setup()
    _L2_gnn_in = {k: v for k, v in _L2_gnn_all.items() if k in ('weight',)}
    del _L2_gnn_all

    def _L3_gnn_setup():
        import jax, jax.numpy as jnp
        import numpy as np
        EPS = 1e-07
        MAX_TANH = 1.0 - 1e-06

        def _norm(v):
            return jnp.maximum(jnp.linalg.norm(v, axis=-1, keepdims=True), EPS)

        def log_map_zero(y):
            n = _norm(y)
            return jnp.arctanh(jnp.clip(n, 0.0, MAX_TANH)) * y / n

        def exp_map_zero(v):
            n = _norm(v)
            return jnp.tanh(n) * v / n

        def h_add(x, y):
            xy = jnp.sum(x * y, axis=-1, keepdims=True)
            x2 = jnp.sum(x * x, axis=-1, keepdims=True)
            y2 = jnp.sum(y * y, axis=-1, keepdims=True)
            num = (1.0 + 2.0 * xy + y2) * x + (1.0 - x2) * y
            den = 1.0 + 2.0 * xy + x2 * y2
            return num / jnp.maximum(den, EPS)

        def h_mul(x, W):
            return exp_map_zero(log_map_zero(x) @ W)
        key = jax.random.key(seed)
        k1, k2, k3, k4 = jax.random.split(key, 4)
        N, F_IN, F_OUT = (4096, 128, 128)
        x = 0.05 * jax.random.normal(k1, (N, F_IN), dtype=jnp.float32)
        a = (jax.random.uniform(k2, (N, N)) < 0.01).astype(jnp.float32)
        adj = a / jnp.maximum(a.sum(axis=1, keepdims=True), 1.0)
        lim_e = np.sqrt(6.0 / (F_IN + F_IN)) * np.sqrt(2.0)
        lim_l = np.sqrt(6.0 / (2 * F_IN + F_OUT)) * np.sqrt(2.0)
        embed = jax.random.uniform(k3, (F_IN, F_IN), minval=-lim_e, maxval=lim_e, dtype=jnp.float32)
        layer = jax.random.uniform(k4, (2 * F_IN, F_OUT), minval=-lim_l, maxval=lim_l, dtype=jnp.float32)
        embed_bias = jnp.zeros((F_IN,), dtype=jnp.float32)
        layer_bias = jnp.zeros((F_OUT,), dtype=jnp.float32)
        return {'x': x, 'adj': adj, 'embed': embed, 'layer': layer, 'embed_bias': embed_bias, 'layer_bias': layer_bias}
    _L3_gnn_all = _L3_gnn_setup()
    _L3_gnn_in = {k: v for k, v in _L3_gnn_all.items() if k in ('embed', 'layer', 'embed_bias', 'layer_bias')}
    del _L3_gnn_all
    return {'x': x, 'adj': adj, 'L0_gnn_W': _L0_gnn_in['W'], 'L0_gnn_b': _L0_gnn_in['b'], 'L1_gnn_inlayer2': _L1_gnn_in['inlayer2'], 'L1_gnn_W1': _L1_gnn_in['W1'], 'L1_gnn_w2': _L1_gnn_in['w2'], 'L1_gnn_b2': _L1_gnn_in['b2'], 'L1_gnn_w3': _L1_gnn_in['w3'], 'L1_gnn_b3': _L1_gnn_in['b3'], 'L2_gnn_weight': _L2_gnn_in['weight'], 'L3_gnn_embed': _L3_gnn_in['embed'], 'L3_gnn_layer': _L3_gnn_in['layer'], 'L3_gnn_embed_bias': _L3_gnn_in['embed_bias'], 'L3_gnn_layer_bias': _L3_gnn_in['layer_bias']}

def reference(x, adj, L0_gnn_W, L0_gnn_b, L1_gnn_inlayer2, L1_gnn_W1, L1_gnn_w2, L1_gnn_b2, L1_gnn_w3, L1_gnn_b3, L2_gnn_weight, L3_gnn_embed, L3_gnn_layer, L3_gnn_embed_bias, L3_gnn_layer_bias):
    import jax
    import jax.numpy as jnp

    def _L0_gnn_ref(X, adj, W, b):
        import jax, jax.numpy as jnp
        import numpy as np
        N = 8192
        C = 128
        F = 128
        adj_hat = adj + jnp.eye(adj.shape[0], dtype=adj.dtype)
        d_inv_sqrt = 1.0 / jnp.sqrt(jnp.sum(adj_hat, axis=1))
        adj_norm = adj_hat * d_inv_sqrt[:, None] * d_inv_sqrt[None, :]
        out = adj_norm @ (X @ W) + b
        return jax.nn.relu(out)

    def _L1_gnn_ref(inlayer, inlayer2, adj_mat, W1, w2, b2, w3, b3):
        import jax, jax.numpy as jnp
        import numpy as np
        N, EMB, HID = (4096, 128, 128)
        in_fts = jnp.einsum('ne,he->nh', inlayer2, W1)
        f1 = in_fts @ w2 + b2
        f2 = in_fts @ w3 + b3
        logits = f1[:, None] + f2[None, :]
        logits = adj_mat * logits
        bias_mat = -1000000000.0 * (1.0 - (adj_mat > 0).astype(jnp.float32))
        coefs = jax.nn.softmax(jax.nn.leaky_relu(logits, 0.01) + bias_mat, axis=1)
        vals = coefs @ inlayer
        return vals

    def _L2_gnn_ref(x, adj, weight):
        import jax, jax.numpy as jnp
        import numpy as np
        N = 4096
        F = 128
        n = adj.shape[0]
        adj_hat = adj + jnp.eye(n, dtype=adj.dtype)
        deg = jnp.sum(adj_hat, axis=1)
        d_inv_sqrt = (deg + 1e-08) ** (-0.5)
        support = d_inv_sqrt[:, None] * adj_hat * d_inv_sqrt[None, :]
        out = jnp.matmul(jnp.matmul(support, x), weight)
        return jax.nn.relu(out)

    def _L3_gnn_ref(x, adj, embed, layer, embed_bias, layer_bias):
        import jax, jax.numpy as jnp
        import numpy as np
        EPS = 1e-07
        MAX_TANH = 1.0 - 1e-06

        def _norm(v):
            return jnp.maximum(jnp.linalg.norm(v, axis=-1, keepdims=True), EPS)

        def log_map_zero(y):
            n = _norm(y)
            return jnp.arctanh(jnp.clip(n, 0.0, MAX_TANH)) * y / n

        def exp_map_zero(v):
            n = _norm(v)
            return jnp.tanh(n) * v / n

        def h_add(x, y):
            xy = jnp.sum(x * y, axis=-1, keepdims=True)
            x2 = jnp.sum(x * x, axis=-1, keepdims=True)
            y2 = jnp.sum(y * y, axis=-1, keepdims=True)
            num = (1.0 + 2.0 * xy + y2) * x + (1.0 - x2) * y
            den = 1.0 + 2.0 * xy + x2 * y2
            return num / jnp.maximum(den, EPS)

        def h_mul(x, W):
            return exp_map_zero(log_map_zero(x) @ W)
        h = h_mul(x, embed)
        h = h_add(h, embed_bias[None, :])
        neigh = exp_map_zero(adj @ log_map_zero(h))
        out = h_mul(jnp.concatenate((x, neigh), axis=1), layer)
        out = h_add(out, layer_bias[None, :])
        return out
    h = jnp.maximum(_layernorm(x, axis=-1), 0.0)
    x = x + _L0_gnn_ref(h, adj, L0_gnn_W, L0_gnn_b)
    h = jnp.maximum(_layernorm(x, axis=-1), 0.0)
    x = x + _L1_gnn_ref(h, L1_gnn_inlayer2, adj, L1_gnn_W1, L1_gnn_w2, L1_gnn_b2, L1_gnn_w3, L1_gnn_b3)
    h = jnp.maximum(_layernorm(x, axis=-1), 0.0)
    x = x + _L2_gnn_ref(h, adj, L2_gnn_weight)
    h = jnp.maximum(_layernorm(x, axis=-1), 0.0)
    x = x + _L3_gnn_ref(h, adj, L3_gnn_embed, L3_gnn_layer, L3_gnn_embed_bias, L3_gnn_layer_bias)
    return x

_drawn_inputs = setup_inputs


def setup_inputs(seed=0):
    import zlib

    import numpy as np

    out = dict(_drawn_inputs(seed))
    spreads = {'L3_gnn_embed_bias': (0.0, 0.1), 'L3_gnn_layer_bias': (0.0, 0.1)}
    factors = {}
    for name, (base, spread) in spreads.items():
        noise = np.random.default_rng([zlib.crc32(name.encode()), seed]).standard_normal(out[name].shape)
        drawn = base * np.exp(spread * noise) if base else spread * noise
        out[name] = jnp.asarray(drawn.astype(out[name].dtype))
    for name, factor in factors.items():
        out[name] = (out[name] * factor).astype(out[name].dtype)
    return out
```

```python
import itertools
from contextlib import ExitStack

import concourse.bass as bass
from concourse import mybir

F32 = mybir.dt.float32
F32R = mybir.dt.float32r
BF16 = mybir.dt.bfloat16
ALU = mybir.AluOpType
ACT = mybir.ActivationFunctionType
AX = mybir.AxisListType

P = 128
N = 4096
F = 128
TILES = N // P
R4 = 4
ROWS = R4 * P
BLOCKS = N // ROWS
QUARTERS = 4
QCOLS = N // QUARTERS
QT = QCOLS // P
HALF = N // 2
LAG = 3
BUFS = 4
STEPS = BLOCKS * TILES
LN_EPS = 1e-5
DEG_EPS = 1e-8
H_EPS = 1e-7
MAX_TANH = 1.0 - 1e-6
MASKED = -1e9
SLOPE = 0.01
SPARES = 16
GROUPS = TILES // R4
ESTEPS = TILES * GROUPS


def build(nc, x_d, adj_d, w0_d, b0_d, in2_d, w1_d, w2_d, b2_d, w3_d, b3_d, wg2_d, emb_d, lay_d, eb_d, lb_d, out_d):
    ctx = ExitStack()
    with ctx:
        def sb(name, shape, dt=F32):
            return ctx.enter_context(nc.sbuf_tensor(name, shape, dt))

        def sem(name):
            return ctx.enter_context(nc.semaphore(name))

        X = sb("X", [P, TILES, F])
        H = sb("H", [P, TILES, F])
        YA = [sb("YA_hi", [P, TILES, F], F32R), sb("YA_lo", [P, TILES, F], F32R)]
        ring = sb("ring", [P, 4, N])
        quarter = [ring[:, c, :].rearrange("p (r m) -> p r m", r=R4) for c in range(QUARTERS)]
        xw = sb("xw", [P, R4, F])
        yw = sb("yw", [P, R4, F])
        hw = sb("hw", [P, R4, F])
        early = ExitStack()
        ones = early.enter_context(nc.sbuf_tensor("ones", [P, P], F32))
        W1 = early.enter_context(nc.sbuf_tensor("W1", [P, 2 * F], F32))
        u3B = early.enter_context(nc.sbuf_tensor("u3B", [P, 2, P], F32))
        early.close()
        hv = sb("hv", [P, R4, F])
        tw = sb("tw", [P, R4, F])
        hT = tw[:, :, :].rearrange("p r n -> p (r n)")
        oT = [sb(f"oT{e}", [P, ROWS]) for e in range(2)]
        stage_hi = sb("stage_hi", [P, R4, F], F32R)
        stage_lo = sb("stage_lo", [P, R4, F], F32R)
        pq = sb("pq", [P, R4, 2 * F])
        sink = sb("sink", [P, R4, F], BF16)
        sink2 = sb("sink2", [P, R4, F], BF16)
        idf = sb("idf", [P, P])
        idr = sb("idr", [P, P], F32R)
        W0 = sb("W0", [P, F])
        W2 = sb("W2", [P, F])
        EL = sb("EL", [P, 2 * F])
        IL = sb("IL", [P, 2 * F])
        w23 = sb("w23", [P, 2])
        u23 = sb("u23", [P, 2, 2])
        b0B = sb("b0B", [P, F])
        eB = sb("eB", [P, F])
        lB = sb("lB", [P, F])
        b23 = sb("b23", [P, 2])
        y2 = sb("y2", [P, 2])
        nhalf = sb("nhalf", [P, TILES])
        half = sb("half", [P, R4])
        mone = sb("mone", [P, R4])
        deg = sb("deg", [P, TILES])
        deg2 = sb("deg2", [P, TILES])
        d0 = sb("d0", [P, TILES])
        d2 = sb("d2", [P, TILES])
        f1 = sb("f1", [P, TILES])
        nh2 = sb("nh2", [P, TILES])
        dpart = sb("dpart", [P, QUARTERS, R4])
        st = sb("st", [P, R4, 6])
        mv = sb("mv", [P, R4, 2])
        ve = sb("ve", [P, R4])
        rs = sb("rs", [P, R4])
        mx = sb("mx", [P, 2])
        negm = sb("negm", [P, 2])
        rsum = sb("rsum", [P, 2, R4])
        rcp = sb("rcp", [P, R4])
        sq1 = sb("sq1", [P, R4])
        sq2 = sb("sq2", [P, R4])
        sq3 = sb("sq3", [P, R4])
        dot = sb("dot", [P, R4])
        ln1 = sb("ln1", [P, R4])
        ln2 = sb("ln2", [P, R4])
        th = sb("th", [P, R4])
        nrm = sb("nrm", [P, R4])
        nrc = sb("nrc", [P, R4])
        nth = sb("nth", [P, R4])
        sc0 = sb("sc0", [P, R4])
        sc1 = sb("sc1", [P, R4])
        al = sb("al", [P, R4])
        be = sb("be", [P, R4])
        ps = sb("ps", [P, 8, R4])
        spare = sb("spare", [P, 3, SPARES])

        early = ExitStack()
        in2 = early.enter_context(nc.sbuf_tensor("in2", [P, 2, R4, 2 * F], F32))
        in2T = early.enter_context(nc.sbuf_tensor("in2T", [P, 2, 2, ROWS], F32))
        early.close()
        early = ExitStack()
        ET = early.enter_context(nc.sbuf_tensor("ET", [P, BUFS, R4, P], F32))
        early.close()
        hi = sb("hi", [P, BUFS, ROWS], F32R)
        lo = sb("lo", [P, BUFS, ROWS], F32R)
        early = ExitStack()
        f2B = early.enter_context(nc.sbuf_tensor("f2B", [P, N], F32))
        R = early.enter_context(nc.sbuf_tensor("R", [P, 2, HALF], F32))
        early.close()
        YB = [sb("YB_hi", [P, TILES, F], F32R), sb("YB_lo", [P, TILES, F], F32R)]
        FEATURES = [YA, YA, YB]

        TP = [ctx.enter_context(nc.psum_tensor(f"TP{i}", [P, ROWS], F32)) for i in range(BUFS)]
        OT = [ctx.enter_context(nc.psum_tensor(f"OT{i}", [P, ROWS], F32)) for i in range(2)]
        PP = ctx.enter_context(nc.psum_tensor("PP", [P, 2, ROWS], F32))
        PQ = PP[:, :, :].rearrange("p a (r n) -> p (a r) n", n=2 * F)

        consts_in = sem("consts_in")
        x_in = sem("x_in")
        in2_in = [sem(f"in2_in{i}") for i in range(2)]
        adj_in = [sem(f"adj_in{i}") for i in range(4)]
        consts = sem("consts")
        ident = sem("ident")
        ident_r = sem("ident_r")
        u_done = sem("u_done")
        u_copied = sem("u_copied")
        u_spread = sem("u_spread")
        y2_done = sem("y2_done")
        in2_turned = sem("in2_turned")
        in2_copied = sem("in2_copied")
        f_done = sem("f_done")
        f_copied = sem("f_copied")
        summed = sem("summed")
        deg_ready = sem("deg_ready")
        d_step = sem("d_step")
        d_ready = sem("d_ready")
        x_new = sem("x_new")
        x_kept = sem("x_kept")
        bn_stat = sem("bn_stat")
        bn_agg = sem("bn_agg")
        var_ready = sem("var_ready")
        pow_done = sem("pow_done")
        rstd_ready = sem("rstd_ready")
        normed = sem("normed")
        h_ready = sem("h_ready")
        y0_scaled = sem("y0_scaled")
        yhi_ready = sem("yhi_ready")
        y_ready = sem("y_ready")
        turned = sem("turned")
        hi_done = sem("hi_done")
        lo_done = sem("lo_done")
        spent = sem("spent")
        staged = sem("staged")
        oT_ready = sem("oT_ready")
        post_done = sem("post_done")
        scaled = sem("scaled")
        biased0 = sem("biased0")
        neg_step = sem("neg_step")
        multiplied = sem("multiplied")
        biased = sem("biased")
        masked = sem("masked")
        m_ready = sem("m_ready")
        exp_done = sem("exp_done")
        et_turned = sem("et_turned")
        et_copied = sem("et_copied")
        et_used = sem("et_used")
        l1_out = sem("l1_out")
        l1_taken = sem("l1_taken")
        rcp_ready = sem("rcp_ready")
        hw_ready = sem("hw_ready")
        hT_turned = sem("hT_turned")
        hT_ready = sem("hT_ready")
        pq_done = sem("pq_done")
        pq_ready = sem("pq_ready")
        pq_used = sem("pq_used")
        q_kept = sem("q_kept")
        sq1_ready = sem("sq1_ready")
        sq2_ready = sem("sq2_ready")
        sq3_ready = sem("sq3_ready")
        dot_ready = sem("dot_ready")
        nrm_ready = sem("nrm_ready")
        ln_ready = sem("ln_ready")
        nth_ready = sem("nth_ready")
        th_ready = sem("th_ready")
        coef_ready = sem("coef_ready")
        mix_ready = sem("mix_ready")
        mixed = sem("mixed")
        w_ready = sem("w_ready")
        s_ready = sem("s_ready")
        pool_step = sem("pool_step")
        bias_scaled = sem("bias_scaled")
        w_scaled = sem("w_scaled")
        y3_scaled = sem("y3_scaled")
        nh2_kept = sem("nh2_kept")
        il_ready = sem("il_ready")
        x_final = sem("x_final")
        stored = sem("stored")

        block = ctx.enter_context(nc.Block())

        QUARTER_USES = [[BLOCKS] * 4,
                        [2 * BLOCKS + TILES // 2] * 2 + [2 * BLOCKS] * 2,
                        [3 * BLOCKS + TILES // 2] * 2 + [3 * BLOCKS] * 2]
        ROWTILE_USES = 2 * BLOCKS
        CONST_DMAS = 13
        PER2 = 63
        PER3 = 47

        def tiles_of(t, s):
            return t[:, bass.ds(s * R4, R4), :]

        def cols_of(t, s):
            return t[:, bass.ds(s * R4, R4)]

        def per_row(t):
            return t.rearrange("p (r o) -> p r o", o=1).to_broadcast([P, R4, F])

        def per_col(t):
            return t.rearrange("p (o n) -> p o n", o=1).to_broadcast([P, R4, F])

        def spare_column(e):
            return (spare[:, e, i:i + 1] for i in itertools.cycle(range(SPARES)))

        def settle(carrier, s, value):
            eng, carry = carrier
            eng.wait_ge(s, value)
            if not isinstance(value, int):
                carry()

        def blocks_loop(eng, body):
            body(0, True)
            with eng.Fori(1, BLOCKS // 2) as q:
                body(q, False)

        @block.sync
        def _(sp):
            sp.dma_start(X[:, :, :], x_d.rearrange("(t p) f -> p t f", p=P)).then_inc(x_in, 16)

            def load(s, c):
                sp.dma_start(quarter[c], adj_d[bass.ds(s * ROWS, ROWS), c * QCOLS:(c + 1) * QCOLS]
                             .rearrange("(r p) m -> p r m", p=P)).then_inc(adj_in[c], 16)

            def load_pass(base, after):
                for c in range(QUARTERS):
                    after(c)
                    load(0, c)
                with sp.Fori(1, BLOCKS) as s:
                    for c in range(QUARTERS):
                        sp.wait_ge(turned, s * TILES + (base - TILES + QT * (c + 1)))
                        load(s, c)

            for c in range(QUARTERS):
                load(0, c)
            with sp.Fori(1, BLOCKS) as s:
                for c in range(QUARTERS):
                    sp.wait_ge(summed, s * 4 + (c - 3))
                    load(s, c)
            load_pass(0, lambda c: sp.wait_ge(summed, 4 * (BLOCKS - 1) + c + 1))
            for e in range(2):
                sp.wait_ge(turned, STEPS - TILES + QT * (e + 1))
                sp.dma_start(ring[:, e, :], adj_d[e * P:(e + 1) * P, :]).then_inc(adj_in[e], 16)
            with sp.Fori(1, TILES // 2) as u:
                for e in range(2):
                    sp.wait_ge(biased, u * 4 + (2 * e - 2))
                    sp.dma_start(ring[:, e, :], adj_d[bass.ds(u * (2 * P) + e * P, P), :]).then_inc(adj_in[e], 16)

            def after_layer1(c):
                if c < 2:
                    sp.wait_ge(biased, 2 * (TILES - 2 + c + 1))
                else:
                    sp.wait_ge(et_turned, ESTEPS - GROUPS * (3 - c))
            load_pass(STEPS, after_layer1)
            load_pass(2 * STEPS, lambda c: sp.wait_ge(turned, 2 * STEPS - TILES + QT * (c + 1)))
            out_v = out_d.rearrange("(t p) f -> p t f", p=P)
            for s in range(BLOCKS):
                sp.wait_ge(x_final, s + 1)
                sp.dma_start(out_v[:, s * R4:(s + 1) * R4, :], X[:, s * R4:(s + 1) * R4, :]).then_inc(stored, 16)
            sp.wait_ge(stored, 16 * BLOCKS)

        @block.tensor
        def _(pe):
            pe.wait_ge(ident, 2)
            pe.wait_ge(il_ready, 1)
            pe.wait_ge(consts_in, 16 * CONST_DMAS)
            for k in range(2):
                mm = pe.matmul(PP[:, 1, 2 * k:2 * k + 2], W1[:, k * F:(k + 1) * F], w23[:, :], start=True, stop=True)
            mm.then_inc(u_done, 1)
            pe.wait_ge(u_spread, 1)

            def attention_sums(q, first):
                for e in range(2):
                    s = q * 2 + e
                    pe.wait_ge(in2_in[e], q * 16 + 16)
                    for k in range(2):
                        if not first:
                            pe.wait_ge(in2_copied, s * 2 + (k - 3))
                        for r in range(R4):
                            mm = pe.transpose(TP[2 * e + k][:, r * P:(r + 1) * P], in2[:, e, r, k * P:(k + 1) * P],
                                              idf[:, :])
                        mm.then_inc(in2_turned, 1)
                    pe.wait_ge(in2_copied, s * 2 + 2)
                    if not first:
                        pe.wait_ge(f_copied, s * 2 - 2)
                    for k in range(2):
                        pe.matmul(OT[e][:, :], u3B[:, k, :], in2T[:, e, k, :], start=(k == 0), stop=(k == 1))
                    for r in range(R4):
                        for k in range(2):
                            mm = pe.matmul(PP[:, e, 16 + r:17 + r], in2T[:, e, k, r * P:(r + 1) * P],
                                           u23[:, k, 0:1], start=(k == 0), stop=(k == 1))
                    mm.then_inc(f_done, 1)

            blocks_loop(pe, attention_sums)

            def turn(p, s, j):
                c = j // QT
                if j % QT == 0:
                    pe.wait_ge(adj_in[c], s * 16 + 16 * (QUARTER_USES[p][c] + 1))
                for r in range(R4):
                    mm = pe.transpose(TP[j % BUFS][:, r * P:(r + 1) * P],
                                      quarter[c][:, r, (j % QT) * P:(j % QT + 1) * P], idf[:, :])
                mm.then_inc(turned, 1)

            def product(p, s, e, j, first_block):
                y_hi, y_lo = FEATURES[p]
                if first_block and j % R4 == 0:
                    pe.wait_ge(y_ready, p * BLOCKS + j // R4 + 1)
                if j == 0:
                    if p == 0 and first_block:
                        pe.wait_ge(f_copied, 2 * BLOCKS)
                    elif p == 1 and first_block:
                        pe.wait_ge(l1_taken, BLOCKS - 1 + e)
                    else:
                        pe.wait_ge(oT_ready, s + (p * BLOCKS - 1))
                pe.wait_ge(lo_done, s * TILES + (p * STEPS + j + 1))
                if p < 2 and j == TILES - 1:
                    pe.wait_ge(staged, s + (p * BLOCKS + 1))
                    for r in range(R4):
                        for part in (stage_hi, stage_lo):
                            pe.matmul(OT[e][:, r * P:(r + 1) * P], part[:, r, :], idr[:, :], start=False, stop=False,
                                      skip_group_check=True)
                a_hi, a_lo = hi[:, j % BUFS, :], lo[:, j % BUFS, :]
                pe.matmul(OT[e][:, :], y_hi[:, j, :], a_hi, start=(j == 0), stop=False)
                pe.matmul(OT[e][:, :], y_hi[:, j, :], a_lo, start=False, stop=False)
                pe.matmul(OT[e][:, :], y_lo[:, j, :], a_hi, start=False, stop=(j == TILES - 1)).then_inc(spent, 1)

            def weigh(p, s, e):
                pe.wait_ge(oT_ready, s + (p * BLOCKS + 1))
                if p == 0:
                    if isinstance(s, int) and s == 0:
                        pe.wait_ge(f_copied, 2 * BLOCKS)
                    else:
                        pe.wait_ge(scaled, s)
                else:
                    if not (p == 1 and isinstance(s, int) and s == 0):
                        pe.wait_ge(pq_ready, s + (p - 1) * BLOCKS)
                for r in range(R4):
                    if p < 2:
                        mm = pe.matmul(PP[:, 0, r * P:(r + 1) * P], oT[e][:, r * P:(r + 1) * P],
                                       (W0, W2)[p][:, :], start=True, stop=True)
                    else:
                        mm = pe.matmul(PQ[:, r, :], oT[e][:, r * P:(r + 1) * P], IL[:, :], start=True, stop=True)
                mm.then_inc(post_done, 1)

            def turn_h(s):
                pe.wait_ge(hw_ready, s + 1)
                for r in range(R4):
                    mm = pe.transpose(PP[:, 1, r * P:(r + 1) * P], hw[:, r, :], idf[:, :])
                mm.then_inc(hT_turned, 1)

            def embed_h(s):
                pe.wait_ge(hT_ready, s + 1)
                for r in range(R4):
                    mm = pe.matmul(PQ[:, r, :], hT[:, r * P:(r + 1) * P], EL[:, :], start=True, stop=True)
                mm.then_inc(pq_done, 1)

            def gcn_pass(p):
                def body(q, first):
                    for k in range(2 * TILES):
                        e, j = divmod(k, TILES)
                        turn(p, q * 2 + e, j)
                        if k >= LAG:
                            e2, j2 = divmod(k - LAG, TILES)
                            product(p, q * 2 + e2, e2, j2, first and e2 == 0)
                        elif not first:
                            product(p, q * 2 - 1, 1, TILES + k - LAG, False)
                        if not (first and e == 0):
                            if j == 5:
                                weigh(p, q * 2 + (e - 1), 1 - e)
                            if p == 1 and j == 11:
                                turn_h(q * 2 + (e - 1))
                            if p == 1 and j == 13:
                                embed_h(q * 2 + (e - 1))

                blocks_loop(pe, body)
                for j in range(TILES - LAG, TILES):
                    product(p, BLOCKS - 1, 1, j, False)
                weigh(p, BLOCKS - 1, 1)
                if p == 1:
                    turn_h(BLOCKS - 1)
                    embed_h(BLOCKS - 1)

            pe.wait_ge(ident_r, 1)
            gcn_pass(0)

            def turn_e(t, i, g):
                if g == 0:
                    pe.wait_ge(exp_done, t + 1)
                for k in range(R4):
                    mm = pe.transpose(TP[g % BUFS][:, k * P:(k + 1) * P],
                                      ring[:, 2 + i % 2, (g * R4 + k) * P:(g * R4 + k + 1) * P], idf[:, :])
                mm.then_inc(et_turned, 1)

            def product_e(t, s, i, g, first_tile, first):
                if first_tile:
                    pe.wait_ge(h_ready, BLOCKS + g + 1)
                if i % R4 == 0 and g == 0:
                    if first:
                        pe.wait_ge(oT_ready, BLOCKS - 1 + i // R4)
                    else:
                        pe.wait_ge(l1_taken, s - 1)
                pe.wait_ge(et_copied, t * GROUPS + (g + 1))
                r = i % R4
                for k in range(R4):
                    mm = pe.matmul(OT[i // R4][:, r * P:(r + 1) * P], ET[:, g % BUFS, k, :], H[:, g * R4 + k, :],
                                   start=(g == 0 and k == 0), stop=(g == GROUPS - 1 and k == R4 - 1))
                mm.then_inc(et_used, 1)

            def attend(q, first):
                for i in range(2 * R4):
                    for g in range(GROUPS):
                        turn_e(q * 8 + i, i, g)
                        i2, g2 = (i, g - 2) if g >= 2 else (i - 1, g + GROUPS - 2)
                        if i2 >= 0:
                            product_e(q * 8 + i2, q * 2 + i2 // R4, i2, g2, first and i2 == 0, first)
                        elif not first:
                            product_e(q * 8 - 1, q * 2 - 1, 7, g2, False, False)

            blocks_loop(pe, attend)
            for g in range(GROUPS - 2, GROUPS):
                product_e(TILES - 1, BLOCKS - 1, 7, g, False, False)

            gcn_pass(1)
            gcn_pass(2)

        @block.scalar
        def _(act):
            act_spare = spare_column(0)
            act_carry = (act, lambda: act.activation(next(act_spare), nhalf[:, 0:1], ACT.Copy))
            for dst, src in ((W0, w0_d), (W2, wg2_d), (EL[:, 0:F], emb_d), (EL[:, F:2 * F], lay_d[0:F, :]),
                             (IL[:, F:2 * F], lay_d[F:2 * F, :]), (W1, w1_d),
                             (w23[:, 0:1], w2_d.rearrange("(n a) -> n a", a=1)),
                             (w23[:, 1:2], w3_d.rearrange("(n a) -> n a", a=1)),
                             (b0B, b0_d.rearrange("(a n) -> a n", a=1).to_broadcast([P, F])),
                             (eB, eb_d.rearrange("(a n) -> a n", a=1).to_broadcast([P, F])),
                             (lB, lb_d.rearrange("(a n) -> a n", a=1).to_broadcast([P, F])),
                             (b23[:, 0:1], b2_d.rearrange("(a n) -> a n", a=1).to_broadcast([P, 1])),
                             (b23[:, 1:2], b3_d.rearrange("(a n) -> a n", a=1).to_broadcast([P, 1]))):
                act.dma_start(dst[:, :], src).then_inc(consts_in, 16)
            act.dma_start(in2[:, 0, :, :], in2_d[0:ROWS, :].rearrange("(r p) m -> p r m", p=P)).then_inc(in2_in[0], 16)
            act.dma_start(in2[:, 1, :, :], in2_d[ROWS:2 * ROWS, :].rearrange("(r p) m -> p r m", p=P))\
               .then_inc(in2_in[1], 16)
            act.wait_ge(ident, 2)
            act.activation(idr[:, :], idf[:, :], ACT.Copy).then_inc(ident_r, 1)
            act.wait_ge(u_done, 1)
            act.activation(u23[:, :, :].rearrange("p a b -> p (a b)"), PP[:, 1, 0:4], ACT.Copy).then_inc(u_copied, 1)
            act.wait_ge(u_copied, 1)
            act.wait_ge(consts, 4)
            act.activation(u3B[:, 0, :], ones[:, :], ACT.Copy, scale=u23[:, 0, 1:2])
            act.activation(u3B[:, 1, :], ones[:, :], ACT.Copy, scale=u23[:, 1, 1:2]).then_inc(u_spread, 1)
            act.wait_ge(consts_in, 16 * CONST_DMAS)
            act.activation(sink[:, 0, :], eB[:, :], ACT.Square, accum_out=y2[:, 0:1]).then_inc(y2_done, 1)
            act.wait_ge(y2_done, 1)
            act.activation(sink[:, 1, :], lB[:, :], ACT.Square, accum_out=y2[:, 1:2]).then_inc(y2_done, 1)

            def attention_sums(q, first):
                for e in range(2):
                    s = q * 2 + e
                    for k in range(2):
                        act.wait_ge(in2_turned, s * 2 + (k + 1))
                        act.activation(in2T[:, e, k, :], TP[2 * e + k][:, :], ACT.Copy).then_inc(in2_copied, 1)
                    settle(act_carry, f_done, s + 1)
                    act.activation(f2B[:, bass.ds(s * ROWS, ROWS)], OT[e][:, :], ACT.Identity, bias=b23[:, 1:2])\
                       .then_inc(f_copied, 1)
                    act.activation(cols_of(f1, s), PP[:, e, 16:20], ACT.Identity, bias=b23[:, 0:1])\
                       .then_inc(f_copied, 1)

            def load_in2(s, e):
                act.dma_start(in2[:, e, :, :], in2_d[bass.ds(s * ROWS, ROWS), :].rearrange("(r p) m -> p r m", p=P))\
                   .then_inc(in2_in[e], 16)

            attention_sums(0, True)
            with act.Fori(1, BLOCKS // 2) as q:
                for e in range(2):
                    load_in2(q * 2 + e, e)
                attention_sums(q, False)

            def split_hi(p, s, j, first):
                act.wait_ge(turned, s * TILES + (p * STEPS + j + 1))
                if first and j < BUFS:
                    if p == 0:
                        act.wait_ge(f_done, BLOCKS)
                    elif p == 1:
                        act.wait_ge(et_used, ESTEPS)
                    else:
                        act.wait_ge(spent, p * STEPS + j - BUFS + 1)
                else:
                    act.wait_ge(spent, s * TILES + (p * STEPS + j - BUFS + 1))
                act.activation(hi[:, j % BUFS, :], TP[j % BUFS][:, :], ACT.Copy).then_inc(hi_done, 1)

            def take_sums(p, s, e):
                act.wait_ge(spent, s * TILES + (p * STEPS + TILES))
                act.activation(oT[e][:, :], OT[e][:, :], ACT.Copy).then_inc(oT_ready, 1)

            def squares(src, dst, ready):
                for r in range(R4):
                    ins = act.activation(sink[:, r, :], src[:, r, 0:F], ACT.Square, accum_out=dst[:, r:r + 1])
                ins.then_inc(ready, 1)

            def take_hT(s):
                act.wait_ge(hT_turned, s + 1)
                act.activation(hT, PP[:, 1, :], ACT.Copy).then_inc(hT_ready, 1)

            def take_pq(p, s):
                if p == 1:
                    act.wait_ge(pq_done, s + 1)
                else:
                    act.wait_ge(post_done, s + (2 * BLOCKS + 1))
                if not (p == 1 and isinstance(s, int) and s == 0):
                    act.wait_ge(pq_used, s + (p - 1) * BLOCKS)
                    if p == 1:
                        act.wait_ge(q_kept, s)
                    else:
                        act.wait_ge(q_kept, BLOCKS)
                act.activation(pq[:, :, :], PQ[:, :, :], ACT.Copy).then_inc(pq_ready, 1)

            def logs(n):
                act.wait_ge(nrm_ready, n)
                act.activation(ln1[:, :], nrc[:, :], ACT.Ln, bias=1.0)
                act.activation(ln2[:, :], nrc[:, :], ACT.Ln, bias=1.0, scale=-1.0).then_inc(ln_ready, 1)

            def tanh(n):
                act.wait_ge(nth_ready, n)
                act.activation(th[:, :], nth[:, :], ACT.Tanh).then_inc(th_ready, 1)

            L2_LOGS, L2_TANHS = 2 * BLOCKS, BLOCKS

            def post2(s, j):
                if j == 12:
                    act.wait_ge(hw_ready, s + 1)
                    squares(hw, sq1, sq1_ready)
                    take_hT(s)
                if j == 14:
                    take_pq(1, s)
                    act.wait_ge(pq_ready, s + 1)
                    squares(pq, sq2, sq2_ready)
                if j == 17:
                    logs(s * 2 + 1)
                if j == 20:
                    tanh(s + 1)
                if j == 25:
                    act.wait_ge(mixed, s + 1)
                    squares(hv, sq3, sq3_ready)
                if j == 29:
                    logs(s * 2 + 2)

            def post3(s, j):
                if j == 6:
                    take_pq(2, s)
                    act.wait_ge(pq_ready, s + (BLOCKS + 1))
                    squares(pq, sq1, sq1_ready)
                if j == 10:
                    tanh(s * 2 + (L2_TANHS + 1))
                if j == 14:
                    logs(s + (L2_LOGS + 1))
                if j == 20:
                    act.wait_ge(w_ready, s + 1)
                    squares(hv, sq2, sq2_ready)
                if j == 24:
                    tanh(s * 2 + (L2_TANHS + 2))

            def gcn_pass(p):
                post = (lambda s, j: None, post2, post3)[p]

                def body(q, first):
                    for k in range(2 * TILES):
                        e, j = divmod(k, TILES)
                        split_hi(p, q * 2 + e, j, first and e == 0)
                        if not (first and e == 0):
                            if j == 3:
                                take_sums(p, q * 2 + (e - 1), 1 - e)
                            post(q * 2 + (e - 1), j)

                blocks_loop(act, body)
                take_sums(p, BLOCKS - 1, 1)
                for j in range(TILES):
                    post(BLOCKS - 1, j)

            gcn_pass(0)

            def exps(t, i):
                act.wait_ge(m_ready, t + 1)
                act.activation(ring[:, 2 + i % 2, :], ring[:, 2 + i % 2, :], ACT.Exp, bias=negm[:, i % 2:i % 2 + 1],
                               accum_out=rsum[:, i // R4, i % R4:i % R4 + 1]).then_inc(exp_done, 1)

            def take_e(t, g, first_tile):
                act.wait_ge(et_turned, t * GROUPS + (g + 1))
                if first_tile and g < BUFS:
                    act.wait_ge(spent, STEPS)
                else:
                    act.wait_ge(et_used, t * GROUPS + (g - BUFS + 1))
                act.activation(ET[:, g % BUFS, :, :].rearrange("p k m -> p (k m)"), TP[g % BUFS][:, :], ACT.Copy)\
                   .then_inc(et_copied, 1)

            def attend(q, first):
                for i in range(2 * R4):
                    t = q * 8 + i
                    if not (first and i == 0):
                        exps(t - 1, (i - 1) % 8)
                        for g in range(GROUPS):
                            take_e(t - 1, g, first and i == 1)

            blocks_loop(act, attend)
            exps(TILES - 1, 7)
            for g in range(GROUPS):
                take_e(TILES - 1, g, False)

            gcn_pass(1)
            gcn_pass(2)

        @block.vector
        def _(dve):
            dve_spare = spare_column(1)
            dve_carry = (dve, lambda: dve.memset(next(dve_spare), 0.0))

            def layer_norm(prep, s):
                n = s + (prep * BLOCKS + 1)
                dve.wait_ge(x_new, n)
                for r in range(R4):
                    ins = dve.bn_stats(st[:, r, :], xw[:, r, :])
                ins.then_inc(bn_stat, 1)
                settle(dve_carry, bn_stat, n)
                for r in range(R4):
                    ins = dve.bn_aggr(mv[:, r, :], st[:, r, :])
                ins.then_inc(bn_agg, 1)
                dve.wait_ge(bn_agg, n)
                dve.tensor_scalar(ve[:, :], mv[:, :, 1], LN_EPS, None, ALU.add).then_inc(var_ready, 1)

            def normalise(prep, s):
                n = s + (prep * BLOCKS + 1)
                dve.wait_ge(rstd_ready, n)
                for r in range(R4):
                    ins = dve.tensor_scalar(yw[:, r, :], xw[:, r, :], mv[:, r, 0:1], rs[:, r:r + 1],
                                            ALU.subtract, ALU.mult)
                ins.then_inc(normed, 1)
                dve.wait_ge(normed, n)
                if prep < 2:
                    dve.tensor_scalar(tiles_of(H, s), yw[:, :, :], 0.0, None, ALU.max).then_inc(h_ready, 1)
                elif prep == 2:
                    dve.tensor_scalar(tiles_of(YA[0], s), yw[:, :, :], 0.0, None, ALU.max).then_inc(yhi_ready, 1)
                    dve.wait_ge(yhi_ready, s + (BLOCKS + 1))
                    dve.scalar_tensor_tensor(out=tiles_of(YA[1], s), in0=yw[:, :, :], scalar=0.0,
                                             in1=tiles_of(YA[0], s).bitcast(F32), op0=ALU.max, op1=ALU.subtract)\
                       .then_inc(y_ready, 1)
                else:
                    dve.tensor_scalar(hw[:, :, :], yw[:, :, :], 0.0, None, ALU.max).then_inc(hw_ready, 1)

            dve.wait_ge(x_in, 16)

            def degrees(q, first):
                for e in range(2):
                    s = q * 2 + e
                    for c in range(QUARTERS):
                        dve.wait_ge(adj_in[c], s * 16 + 16)
                        dve.tensor_reduce(dpart[:, c, :], quarter[c], AX.X, ALU.add).then_inc(summed, 1)
                    settle(dve_carry, summed, s * 4 + 4)
                    dve.tensor_reduce(cols_of(deg, s), dpart[:, :, :].rearrange("p c r -> p r c"), AX.X, ALU.add)\
                       .then_inc(deg_ready, 1)
                    dve.tensor_copy(xw[:, :, :], tiles_of(X, s)).then_inc(x_new, 1)
                    layer_norm(0, s)
                    normalise(0, s)

            blocks_loop(dve, degrees)
            dve.wait_ge(d_ready, 1)
            dve.wait_ge(h_ready, BLOCKS)
            for s in range(BLOCKS):
                if s:
                    dve.wait_ge(y_ready, s)
                dve.tensor_tensor(yw[:, :, :], tiles_of(H, s), per_row(cols_of(d0, s)), ALU.mult)\
                   .then_inc(y0_scaled, 1)
                dve.wait_ge(y0_scaled, s + 1)
                dve.tensor_scalar(tiles_of(YA[0], s), yw[:, :, :], 1.0, None, ALU.mult).then_inc(yhi_ready, 1)
                dve.wait_ge(yhi_ready, s + 1)
                dve.tensor_tensor(tiles_of(YA[1], s), yw[:, :, :], tiles_of(YA[0], s).bitcast(F32), ALU.subtract)\
                   .then_inc(y_ready, 1)

            def split_lo(p, s, j):
                dve.wait_ge(hi_done, s * TILES + (p * STEPS + j + 1))
                dve.tensor_tensor(lo[:, j % BUFS, :], TP[j % BUFS][:, :], hi[:, j % BUFS, :].bitcast(F32),
                                  ALU.subtract).then_inc(lo_done, 1)

            def xw_free(prep, s):
                if not (prep == 1 and isinstance(s, int) and s == 0):
                    dve.wait_ge(x_kept, s + (prep - 1) * BLOCKS)

            def post0(s, j):
                if j == 6:
                    dve.wait_ge(post_done, s + 1)
                    dve.wait_ge(h_ready, s + BLOCKS)
                    dve.tensor_tensor(yw[:, :, :], PP[:, 0, :].rearrange("p (r n) -> p r n", r=R4),
                                      per_row(cols_of(d0, s)), ALU.mult).then_inc(scaled, 1)
                    dve.wait_ge(scaled, s + 1)
                    dve.tensor_tensor(yw[:, :, :], yw[:, :, :], per_col(b0B[:, :]), ALU.add).then_inc(biased0, 1)
                if j == 7:
                    dve.wait_ge(biased0, s + 1)
                    xw_free(1, s)
                    dve.scalar_tensor_tensor(out=xw[:, :, :], in0=yw[:, :, :], scalar=0.0, in1=tiles_of(X, s),
                                             op0=ALU.max, op1=ALU.add).then_inc(x_new, 1)
                if j == 9:
                    layer_norm(1, s)
                if j == 12:
                    normalise(1, s)

            def post2(s, j):
                if j == 6:
                    dve.wait_ge(post_done, s + (BLOCKS + 1))
                    dve.scalar_tensor_tensor(out=yw[:, :, :], in0=PP[:, 0, :].rearrange("p (r n) -> p r n", r=R4),
                                             scalar=0.0, in1=per_row(cols_of(d2, s)), op0=ALU.max, op1=ALU.mult)\
                       .then_inc(scaled, 1)
                    dve.wait_ge(scaled, s + (BLOCKS + 1))
                    xw_free(3, s)
                    dve.tensor_tensor(xw[:, :, :], yw[:, :, :], tiles_of(X, s), ALU.add).then_inc(x_new, 1)
                if j == 7:
                    layer_norm(3, s)
                if j == 9:
                    normalise(3, s)
                if j == 15:
                    bias_dot(pq, eB, pq_ready, s + 1)
                if j == 23:
                    mobius(pq[:, :, 0:F], eB, s, s + 1, pq_used)

            def bias_dot(src, bias, ready, n):
                dve.wait_ge(ready, n)
                for r in range(R4):
                    ins = dve.tensor_tensor_reduce(sink2[:, r, :], src[:, r, 0:F], bias[:, :], 1.0, 0.0, ALU.mult,
                                                   ALU.add, dot[:, r:r + 1])
                ins.then_inc(dot_ready, 1)

            def mobius(src, bias, s, n, used):
                dst = hv if used is not None else yw
                dve.wait_ge(mix_ready, n)
                ins = dve.tensor_tensor(dst[:, :, :], src, per_row(al[:, :]), ALU.mult)
                ins.then_inc(used if used is not None else w_scaled, 1)
                dve.tensor_tensor(tw[:, :, :], per_col(bias[:, :]), per_row(be[:, :]), ALU.mult).then_inc(bias_scaled, 1)
                dve.wait_ge(bias_scaled, n)
                dve.tensor_tensor(dst[:, :, :], dst[:, :, :], tw[:, :, :], ALU.add).then_inc(mixed, 1)

            def late2(s):
                dve.wait_ge(s_ready, s + 1)
                dve.tensor_tensor(tw[:, :, :], hv[:, :, :], per_row(sc1[:, :]), ALU.mult).then_inc(y3_scaled, 1)
                dve.wait_ge(y3_scaled, s + 1)
                dve.tensor_scalar(tiles_of(YB[0], s), tw[:, :, :], 1.0, None, ALU.mult).then_inc(yhi_ready, 1)
                dve.wait_ge(yhi_ready, s + (2 * BLOCKS + 1))
                dve.tensor_tensor(tiles_of(YB[1], s), tw[:, :, :], tiles_of(YB[0], s).bitcast(F32), ALU.subtract)\
                   .then_inc(y_ready, 1)

            def post3(s, j):
                if j == 18:
                    dve.wait_ge(coef_ready, s + 1)
                    dve.tensor_tensor(hv[:, :, :], tiles_of(H, s), per_row(sc0[:, :]), ALU.mult)
                    dve.tensor_tensor(tw[:, :, :], pq[:, :, F:2 * F], per_row(sc1[:, :]), ALU.mult)\
                       .then_inc(pq_used, 1)
                    dve.wait_ge(pq_used, s + (BLOCKS + 1))
                    dve.tensor_tensor(hv[:, :, :], hv[:, :, :], tw[:, :, :], ALU.add).then_inc(w_ready, 1)
                if j == 20:
                    bias_dot(hv, lB, w_ready, s + 1)
                if j == 28:
                    mobius(hv[:, :, :], lB, s, s + (BLOCKS + 1), None)
                    dve.wait_ge(mixed, s + (BLOCKS + 1))
                    dve.tensor_tensor(tiles_of(X, s), yw[:, :, :], tiles_of(X, s), ALU.add).then_inc(x_final, 1)

            def gcn_pass(p):
                post = (post0, post2, post3)[p]

                def body(q, first):
                    for k in range(2 * TILES):
                        e, j = divmod(k, TILES)
                        split_lo(p, q * 2 + e, j)
                        if p == 1 and j == 2 and not first:
                            late2(q * 2 + (e - 2))
                        if not (first and e == 0):
                            post(q * 2 + (e - 1), j)

                blocks_loop(dve, body)
                if p == 1:
                    late2(BLOCKS - 2)
                for j in range(TILES):
                    post(BLOCKS - 1, j)
                if p == 1:
                    late2(BLOCKS - 1)

            gcn_pass(0)

            def logits(t, i, first, last_turned):
                a, lg = ring[:, i % 2, :], ring[:, 2 + i % 2, :]
                dve.wait_ge(adj_in[i % 2], (t - i % 2) * 8 + 16 * (ROWTILE_USES + 1))
                last_turned()
                for c in range(2):
                    n = t * 2 + (c + 1)
                    half_of = slice(c * HALF, (c + 1) * HALF)
                    dve.scalar_tensor_tensor(out=lg[:, half_of], in0=f2B[:, half_of], scalar=f1[:, bass.ds(t, 1)],
                                             in1=a[:, half_of], op0=ALU.add, op1=ALU.mult).then_inc(multiplied, 1)
                    dve.tensor_scalar(R[:, c, :], a[:, half_of], 0.0, MASKED / SLOPE, ALU.is_le, ALU.mult)\
                       .then_inc(biased, 1)
                    settle(dve_carry, biased, n)
                    if c == 1:
                        settle(dve_carry, masked, n - 1)
                    dve.tensor_tensor_reduce(lg[:, half_of], lg[:, half_of], R[:, c, :], 1.0,
                                             -3e38 if c == 0 else mx[:, 0:1], ALU.add, ALU.max, mx[:, c:c + 1])\
                       .then_inc(masked, 1)
                dve.wait_ge(masked, t * 2 + 2)
                dve.tensor_scalar(mx[:, 0:1], mx[:, 1:2], -1.0, None, ALU.mult).then_inc(neg_step, 1)
                dve.wait_ge(neg_step, t + 1)
                dve.scalar_tensor_tensor(out=negm[:, i % 2:i % 2 + 1], in0=mx[:, 1:2], scalar=-SLOPE,
                                         in1=mx[:, 0:1], op0=ALU.mult, op1=ALU.min)
                dve.scalar_tensor_tensor(out=lg, in0=lg, scalar=SLOPE, in1=lg, op0=ALU.mult, op1=ALU.max)\
                   .then_inc(m_ready, 1)

            def take_attention(s, e):
                dve.wait_ge(l1_out_step, (s * R4 + R4) * GROUPS)
                dve.reciprocal(rcp[:, :], rsum[:, e, :]).then_inc(rcp_ready, 1)
                dve.wait_ge(rcp_ready, s + 1)
                dve.tensor_tensor(yw[:, :, :], OT[e][:, :].rearrange("p (r n) -> p r n", r=R4), per_row(rcp[:, :]),
                                  ALU.mult).then_inc(l1_taken, 1)
                dve.wait_ge(l1_taken, s + 1)
                xw_free(2, s)
                dve.tensor_tensor(xw[:, :, :], yw[:, :, :], tiles_of(X, s), ALU.add).then_inc(x_new, 1)
                layer_norm(2, s)
                normalise(2, s)

            l1_out_step = et_used

            def attend(q, first):
                for i in range(2 * R4):
                    t = q * 8 + i
                    if first and i < 2:
                        logits(t, i, first, lambda: dve.wait_ge(turned, STEPS))
                    else:
                        logits(t, i, first, lambda: dve.wait_ge(et_turned, t * GROUPS - GROUPS))
                    if i == 1 and not first:
                        take_attention(q * 2 - 1, 1)
                    if i == 5:
                        take_attention(q * 2, 0)

            blocks_loop(dve, attend)
            take_attention(BLOCKS - 1, 1)

            gcn_pass(1)
            gcn_pass(2)

        @block.gpsimd
        def _(pool):
            pool_spare = spare_column(2)

            def idle():
                return pool.tensor_tensor(next(pool_spare), half[:, 0:1], half[:, 0:1], ALU.add)

            pool_carry = (pool, idle)
            pool.memset(idf[:, :], 0.0).then_inc(ident, 1)
            pool.memset(ones[:, :], 1.0).then_inc(consts, 1)
            pool.memset(nhalf[:, :], -0.5).then_inc(consts, 1)
            pool.memset(half[:, :], 0.5).then_inc(consts, 1)
            pool.memset(mone[:, :], -1.0).then_inc(consts, 1)
            pool.wait_ge(ident, 1)
            pool.affine_select(out=idf[:, :], in_=idf[:, :], compare_op=ALU.not_equal, fill=1.0, base=0,
                               pattern=[[-1, P]], channel_multiplier=1).then_inc(ident, 1)
            pool.wait_ge(ident, 2)
            pool.wait_ge(consts, 4)
            pool.tensor_copy(IL[:, 0:F], idf[:, :]).then_inc(il_ready, 1)

            def root(prep, s):
                n = s + (prep * BLOCKS + 1)
                pool.wait_ge(var_ready, n)
                if prep != 2:
                    pool.tensor_tensor(rs[:, :], ve[:, :], nhalf[:, 0:R4], ALU.pow).then_inc(rstd_ready, 1)
                else:
                    pool.tensor_tensor(ps[:, 0, :], ve[:, :], nhalf[:, 0:R4], ALU.pow).then_inc(pow_done, 1)
                    settle(pool_carry, pow_done, s + 1)
                    pool.tensor_tensor(rs[:, :], ps[:, 0, :], cols_of(d2, s), ALU.mult).then_inc(rstd_ready, 1)

            def keep_x(prep, s):
                settle(pool_carry, x_new, s + (prep * BLOCKS + 1))
                pool.tensor_copy(tiles_of(X, s), xw[:, :, :]).then_inc(x_kept, 1)

            with pool.Fori(0, BLOCKS) as s:
                root(0, s)
            pool.wait_ge(deg_ready, BLOCKS)
            pool.tensor_scalar(deg[:, :], deg[:, :], 1.0, None, ALU.add).then_inc(d_step, 1)
            pool.wait_ge(d_step, 1)
            pool.tensor_scalar(deg2[:, :], deg[:, :], DEG_EPS, None, ALU.add).then_inc(d_step, 1)
            pool.tensor_tensor(d0[:, :], deg[:, :], nhalf[:, :], ALU.pow).then_inc(d_ready, 1)
            pool.wait_ge(d_step, 2)
            pool.tensor_tensor(d2[:, :], deg2[:, :], nhalf[:, :], ALU.pow).then_inc(d_ready, 1)
            pool.wait_ge(d_ready, 2)

            def stage(p, s):
                if not (p == 0 and isinstance(s, int) and s == 0):
                    settle(pool_carry, spent, s * TILES + p * STEPS)
                pool.tensor_copy(stage_hi[:, :, :], tiles_of(YA[0], s).bitcast(F32))
                pool.tensor_copy(stage_lo[:, :, :], tiles_of(YA[1], s).bitcast(F32)).then_inc(staged, 1)

            pool.wait_ge(y_ready, BLOCKS)
            stage(0, 0)
            with pool.Fori(1, BLOCKS) as s:
                stage(0, s)
                root(1, s - 1)
                keep_x(1, s - 1)
            root(1, BLOCKS - 1)
            keep_x(1, BLOCKS - 1)

            with pool.Fori(0, BLOCKS) as s:
                root(2, s)
                keep_x(2, s)

            class Chain:

                def __init__(self, base):
                    self.base, self.n = base, 0

                def then(self, ins):
                    ins.then_inc(pool_step, 1)
                    self.n += 1
                    pool.wait_ge(pool_step, self.base + self.n)

                def tt(self, out, a, b, op):
                    self.then(pool.tensor_tensor(out, a, b, op))

                def ts(self, out, a, s1, s2, op0, op1=ALU.bypass):
                    idle()
                    self.then(pool.tensor_scalar(out, a, s1, s2, op0, op1) if s2 is not None
                              else pool.tensor_scalar(out, a, s1, None, op0))

            def bounded_norm(ch, out, square, scale=None):
                ch.tt(out, square, half[:, :], ALU.pow)
                if scale is not None:
                    ch.tt(out, out, scale, ALU.mult)
                ch.ts(out, out, H_EPS, None, ALU.max)

            def log_map(ch, out, n_logs):
                ch.ts(nrc[:, :], nrm[:, :], MAX_TANH, None, ALU.min)
                idle().then_inc(nrm_ready, 1)
                t, p, m, c = (ps[:, i, :] for i in range(4))
                ch.tt(t, nrc[:, :], nrc[:, :], ALU.mult)
                ch.ts(p, t, 1.0 / 9, 1.0 / 7, ALU.mult, ALU.add)
                for k in (1.0 / 5, 1.0 / 3, 1.0):
                    ch.tt(p, p, t, ALU.mult)
                    ch.ts(p, p, k, None, ALU.add)
                ch.ts(m, t, 1.0 / 64, None, ALU.is_lt)
                ch.tt(c, nrc[:, :], mone[:, :], ALU.pow)
                ch.tt(out, nrm[:, :], mone[:, :], ALU.pow)
                ch.tt(out, out, nrc[:, :], ALU.mult)
                pool.wait_ge(ln_ready, n_logs)
                lg = ps[:, 4, :]
                ch.tt(lg, ln1[:, :], ln2[:, :], ALU.subtract)
                ch.tt(lg, lg, half[:, :], ALU.mult)
                ch.tt(lg, lg, c, ALU.mult)
                ch.tt(p, p, lg, ALU.subtract)
                ch.tt(p, p, m, ALU.mult)
                ch.tt(p, p, lg, ALU.add)
                ch.tt(out, out, p, ALU.mult)

            def mix(ch, square, y2c, scale, n_sq, n_dot, n_tanhs):
                pool.wait_ge(sq2_ready, n_sq)
                pool.wait_ge(dot_ready, n_dot)
                bounded_norm(ch, nth[:, :], square, scale)
                idle().then_inc(nth_ready, 1)
                g, xy, x2, a, d = (ps[:, i, :] for i in range(5))
                ch.tt(g, nth[:, :], mone[:, :], ALU.pow)
                if scale is not None:
                    ch.tt(g, g, scale, ALU.mult)
                pool.wait_ge(th_ready, n_tanhs)
                ch.tt(g, g, th[:, :], ALU.mult)
                ch.tt(xy, g, dot[:, :], ALU.mult)
                ch.tt(x2, g, g, ALU.mult)
                ch.tt(x2, x2, square, ALU.mult)
                ch.ts(xy, xy, 2.0, 1.0, ALU.mult, ALU.add)
                yy = y2c.to_broadcast([P, R4])
                ch.tt(a, xy, yy, ALU.add)
                ch.tt(d, x2, yy, ALU.mult)
                ch.tt(d, d, xy, ALU.add)
                ch.ts(d, d, H_EPS, None, ALU.max)
                ch.tt(d, d, mone[:, :], ALU.pow)
                ch.tt(a, a, g, ALU.mult)
                ch.tt(al[:, :], a, d, ALU.mult)
                ch.ts(x2, x2, -1.0, 1.0, ALU.mult, ALU.add)
                ch.tt(be[:, :], x2, d, ALU.mult)
                idle().then_inc(mix_ready, 1)

            def post2(s):
                root(3, s)
                keep_x(3, s)
                settle(pool_carry, pq_ready, s + 1)
                pool.tensor_copy(tiles_of(H, s), pq[:, :, F:2 * F]).then_inc(q_kept, 1)
                settle(pool_carry, sq1_ready, s + 1)
                pool.tensor_copy(cols_of(nh2, s), sq1[:, :]).then_inc(nh2_kept, 1)
                ch = Chain(s * PER2)
                bounded_norm(ch, nrm[:, :], sq1[:, :])
                log_map(ch, sc0[:, :], s * 2 + 1)
                mix(ch, sq2[:, :], y2[:, 0:1], sc0[:, :], s + 1, s + 1, s + 1)
                settle(pool_carry, sq3_ready, s + 1)
                bounded_norm(ch, nrm[:, :], sq3[:, :])
                log_map(ch, sc1[:, :], s * 2 + 2)
                idle().then_inc(s_ready, 1)
                assert ch.n == PER2, ch.n

            def post3(s):
                settle(pool_carry, sq1_ready, s + (BLOCKS + 1))
                ch = Chain(s * PER3 + PER2 * BLOCKS)
                bounded_norm(ch, nth[:, :], sq1[:, :])
                idle().then_inc(nth_ready, 1)
                g, n2 = ps[:, 5, :], ps[:, 6, :]
                ch.tt(g, nth[:, :], mone[:, :], ALU.pow)
                pool.wait_ge(th_ready, s * 2 + (BLOCKS + 1))
                ch.tt(g, g, th[:, :], ALU.mult)
                ch.tt(n2, g, g, ALU.mult)
                ch.tt(n2, n2, sq1[:, :], ALU.mult)
                ch.tt(n2, n2, cols_of(nh2, s), ALU.add)
                bounded_norm(ch, nrm[:, :], n2)
                log_map(ch, sc0[:, :], s + (2 * BLOCKS + 1))
                ch.tt(sc1[:, :], sc0[:, :], g, ALU.mult)
                idle().then_inc(coef_ready, 1)
                mix(ch, sq2[:, :], y2[:, 1:2], None, s + (BLOCKS + 1), s + (BLOCKS + 1), s * 2 + (BLOCKS + 2))
                assert ch.n == PER3, ch.n

            pool.wait_ge(y2_done, 2)
            pool.wait_ge(y_ready, 2 * BLOCKS)
            stage(1, 0)
            with pool.Fori(1, BLOCKS) as s:
                stage(1, s)
                post2(s - 1)
            post2(BLOCKS - 1)
            pool.wait_ge(nh2_kept, BLOCKS)
            with pool.Fori(0, BLOCKS) as s:
                post3(s)


_INS = ['x', 'adj', 'L0_gnn_W', 'L0_gnn_b', 'L1_gnn_inlayer2', 'L1_gnn_W1', 'L1_gnn_w2', 'L1_gnn_b2', 'L1_gnn_w3',
        'L1_gnn_b3', 'L2_gnn_weight', 'L3_gnn_embed', 'L3_gnn_layer', 'L3_gnn_embed_bias', 'L3_gnn_layer_bias']


def kernel(**inputs):
    import numpy as _np
    import concourse.bacc as _bacc
    from concourse import mybir as _mybir
    from concourse.bass_utils import run_bass_kernel_spmd as _run

    nc = _bacc.Bacc("TRN2", target_bir_lowering=False, num_devices=1)
    arrays, args = {}, []
    for name in _INS:
        a = _np.ascontiguousarray(inputs[name])
        if a.ndim == 0:
            a = a.reshape(1)
        arrays[f"in_{name}_dram"] = a
        args.append(nc.dram_tensor(f"in_{name}_dram", a.shape, _mybir.dt.from_np(a.dtype), kind="ExternalInput").ap())
    out = nc.dram_tensor("out_0_dram", (4096, 128), _mybir.dt.float32, kind="ExternalOutput").ap()
    build(nc, *args, out)
    r = _run(nc, [arrays], core_ids=[0])
    return r.results[0]["out_0_dram"]
```

```python
import itertools
from contextlib import ExitStack

import concourse.bass as bass
from concourse import mybir

F32 = mybir.dt.float32
F32R = mybir.dt.float32r
BF16 = mybir.dt.bfloat16
ALU = mybir.AluOpType
ACT = mybir.ActivationFunctionType
AX = mybir.AxisListType

P = 128
N = 4096
F = 128
TILES = N // P
R4 = 4
ROWS = R4 * P
BLOCKS = N // ROWS
QUARTERS = 4
QCOLS = N // QUARTERS
QT = QCOLS // P
HALF = N // 2
LAG = 3
BUFS = 4
STEPS = BLOCKS * TILES
TAKE_SUMS, STAGE, WEIGH = 3, 4, 5
TURN_H, EMBED_H, TAKE_PQ2, LOGS2, DOT2, TANH2, MOBIUS2, LOGS2B, LATE2 = 18, 20, 22, 21, 24, 28, 33, 39, 44
TAKE_PQ3, TANH3, W3, LOGS3, TANH3B, MOBIUS3 = 6, 11, 22, 15, 33, 39
LN_EPS = 1e-5
DEG_EPS = 1e-8
H_EPS = 1e-7
MAX_TANH = 1.0 - 1e-6
MASKED = -1e9
SLOPE = 0.01
SPARES = 12
GROUPS = TILES // R4
ESTEPS = TILES * GROUPS


def build(nc, x_d, adj_d, w0_d, b0_d, in2_d, w1_d, w2_d, b2_d, w3_d, b3_d, wg2_d, emb_d, lay_d, eb_d, lb_d, out_d):
    ctx = ExitStack()
    with ctx:
        def sb(name, shape, dt=F32):
            return ctx.enter_context(nc.sbuf_tensor(name, shape, dt))

        def sem(name):
            return ctx.enter_context(nc.semaphore(name))

        X = sb("X", [P, TILES, F])
        H = sb("H", [P, TILES, F])
        YA = [sb("YA_hi", [P, TILES, F], F32R), sb("YA_lo", [P, TILES, F], F32R)]
        ring = sb("ring", [P, 4, N])
        quarter = [ring[:, c, :].rearrange("p (r m) -> p r m", r=R4) for c in range(QUARTERS)]
        xw = sb("xw", [P, R4, F])
        yw = sb("yw", [P, R4, F])
        hw = sb("hw", [P, R4, F])
        early = ExitStack()
        e_over = early.enter_context(nc.sbuf_tensor("e_over", [P, N], F32))
        early.close()
        early = ExitStack()
        ones = early.enter_context(nc.sbuf_tensor("ones", [P, P], F32))
        W1 = early.enter_context(nc.sbuf_tensor("W1", [P, 2 * F], F32))
        u3B = early.enter_context(nc.sbuf_tensor("u3B", [P, 2, P], F32))
        early.close()
        hv = sb("hv", [P, R4, F])
        tw = sb("tw", [P, R4, F])
        hT = tw[:, :, :].rearrange("p r n -> p (r n)")
        stage_hi = sb("stage_hi", [P, R4, F], F32R)
        stage_lo = sb("stage_lo", [P, R4, F], F32R)
        oT = [sb(f"oT{e}", [P, ROWS]) for e in range(2)]
        pq = sb("pq", [P, R4, 2 * F])
        sink = sb("sink", [P, R4, F], BF16)
        sink2 = sb("sink2", [P, R4, F], BF16)
        idf = sb("idf", [P, P])
        idr = sb("idr", [P, P], F32R)
        W0 = sb("W0", [P, F])
        W2 = sb("W2", [P, F])
        EL = sb("EL", [P, 2 * F])
        IL = sb("IL", [P, 2 * F])
        w23 = sb("w23", [P, 2])
        u23 = sb("u23", [P, 2, 2])
        b0B = sb("b0B", [P, F])
        eB = sb("eB", [P, F])
        lB = sb("lB", [P, F])
        b23 = sb("b23", [P, 2])
        y2 = sb("y2", [P, 2])
        nhalf = sb("nhalf", [P, TILES])
        half = sb("half", [P, R4])
        one = sb("one", [P, R4])
        mone = sb("mone", [P, R4])
        deg = sb("deg", [P, TILES])
        deg2 = sb("deg2", [P, TILES])
        d0 = sb("d0", [P, TILES])
        d2 = sb("d2", [P, TILES])
        f1 = sb("f1", [P, TILES])
        nh2 = sb("nh2", [P, TILES])
        dpart = sb("dpart", [P, QUARTERS, R4])
        st = sb("st", [P, R4, 6])
        mv = sb("mv", [P, R4, 2])
        ve = sb("ve", [P, R4])
        rs = sb("rs", [P, R4])
        mx = sb("mx", [P, 2])
        negm = sb("negm", [P, R4])
        mf1 = sb("mf1", [P, TILES])
        rsum = sb("rsum", [P, 2, 2, R4])
        rcp = sb("rcp", [P, R4])
        sq1 = sb("sq1", [P, R4])
        sq2 = sb("sq2", [P, R4])
        sq3 = sb("sq3", [P, R4])
        dot = sb("dot", [P, R4])
        ln1 = sb("ln1", [P, R4])
        ln2 = sb("ln2", [P, R4])
        th = sb("th", [P, R4])
        nrm = sb("nrm", [P, R4])
        nrc = sb("nrc", [P, R4])
        nth = sb("nth", [P, R4])
        sc0 = sb("sc0", [P, R4])
        sc1 = sb("sc1", [P, R4])
        al = sb("al", [P, R4])
        be = sb("be", [P, R4])
        ps = sb("ps", [P, 8, R4])
        spare = sb("spare", [P, 3, SPARES])

        early = ExitStack()
        in2 = early.enter_context(nc.sbuf_tensor("in2", [P, 2, R4, 2 * F], F32))
        in2T = early.enter_context(nc.sbuf_tensor("in2T", [P, 2, 2, ROWS], F32))
        early.close()
        early = ExitStack()
        ET = early.enter_context(nc.sbuf_tensor("ET", [P, BUFS, R4, P], F32))
        R = early.enter_context(nc.sbuf_tensor("R", [P, HALF], F32))
        early.close()
        hi = sb("hi", [P, BUFS, ROWS], F32R)
        lo = sb("lo", [P, BUFS, ROWS], F32R)
        early = ExitStack()
        f2B = early.enter_context(nc.sbuf_tensor("f2B", [P, N], F32))
        e_beside = early.enter_context(nc.sbuf_tensor("e_beside", [P, N], F32))
        early.close()
        LG = [e_beside[:, :], ring[:, 2, :], ring[:, 3, :], e_over[:, :]]
        YB = [sb("YB_hi", [P, TILES, F], F32R), sb("YB_lo", [P, TILES, F], F32R)]
        FEATURES = [YA, YA, YB]

        TP = [ctx.enter_context(nc.psum_tensor(f"TP{i}", [P, ROWS], F32)) for i in range(BUFS)]
        OT = [ctx.enter_context(nc.psum_tensor(f"OT{i}", [P, ROWS], F32)) for i in range(2)]
        PP = ctx.enter_context(nc.psum_tensor("PP", [P, 2, ROWS], F32))
        PQ = PP[:, :, :].rearrange("p a (r n) -> p (a r) n", n=2 * F)

        consts_in = sem("consts_in")
        x_in = sem("x_in")
        in2_in = [sem(f"in2_in{i}") for i in range(2)]
        adj_in = [sem(f"adj_in{i}") for i in range(4)]
        consts = sem("consts")
        ident = sem("ident")
        ident_r = sem("ident_r")
        u_done = sem("u_done")
        u_copied = sem("u_copied")
        u_spread = sem("u_spread")
        y2_done = sem("y2_done")
        in2_turned = sem("in2_turned")
        in2_copied = sem("in2_copied")
        f_done = sem("f_done")
        f_copied = sem("f_copied")
        summed = sem("summed")
        summed_act = sem("summed_act")
        deg_ready = sem("deg_ready")
        d_step = sem("d_step")
        d_ready = sem("d_ready")
        x_new = sem("x_new")
        x_kept = sem("x_kept")
        stage_part = sem("stage_part")
        bn_stat = sem("bn_stat")
        bn_agg = sem("bn_agg")
        var_ready = sem("var_ready")
        pow_done = sem("pow_done")
        rstd_ready = sem("rstd_ready")
        normed = sem("normed")
        h_ready = sem("h_ready")
        yhi_ready = sem("yhi_ready")
        y_ready = sem("y_ready")
        turned = sem("turned")
        hi_done = sem("hi_done")
        lo_done = sem("lo_done")
        spent = sem("spent")
        staged = sem("staged")
        oT_ready = sem("oT_ready")
        post_done = sem("post_done")
        scaled = sem("scaled")
        biased0 = sem("biased0")
        mf1_ready = sem("mf1_ready")
        bent = sem("bent")
        bent_added = sem("bent_added")
        multiplied = sem("multiplied")
        biased = sem("biased")
        masked = sem("masked")
        m_ready = sem("m_ready")
        exp_done = sem("exp_done")
        et_turned = sem("et_turned")
        et_copied = sem("et_copied")
        et_used = sem("et_used")
        l1_taken = sem("l1_taken")
        rsum_added = sem("rsum_added")
        rcp_ready = sem("rcp_ready")
        hw_ready = sem("hw_ready")
        hT_turned = sem("hT_turned")
        hT_ready = sem("hT_ready")
        pq_done = sem("pq_done")
        pq_ready = sem("pq_ready")
        pq_used = sem("pq_used")
        q_kept = sem("q_kept")
        sq1_ready = sem("sq1_ready")
        sq2_ready = sem("sq2_ready")
        sq3_ready = sem("sq3_ready")
        dot_ready = sem("dot_ready")
        nrm_ready = sem("nrm_ready")
        ln_ready = sem("ln_ready")
        nth_ready = sem("nth_ready")
        th_ready = sem("th_ready")
        coef_ready = sem("coef_ready")
        mix_ready = sem("mix_ready")
        mixed = sem("mixed")
        w_ready = sem("w_ready")
        s_ready = sem("s_ready")
        pool_step = sem("pool_step")
        bias_scaled = sem("bias_scaled")
        w_scaled = sem("w_scaled")
        y3_scaled = sem("y3_scaled")
        nh2_kept = sem("nh2_kept")
        il_ready = sem("il_ready")
        x_final = sem("x_final")
        stored = sem("stored")

        block = ctx.enter_context(nc.Block())

        QUARTER_USES = [[BLOCKS] * 4,
                        [2 * BLOCKS + TILES // 2] * 2 + [2 * BLOCKS] * 2,
                        [3 * BLOCKS + TILES // 2] * 2 + [3 * BLOCKS] * 2]
        ROWTILE_USES = 2 * BLOCKS
        CONST_DMAS = 13
        PER2 = 63
        PER3 = 47

        def tiles_of(t, s):
            return t[:, bass.ds(s * R4, R4), :]

        def cols_of(t, s):
            return t[:, bass.ds(s * R4, R4)]

        def per_row(t):
            return t.rearrange("p (r o) -> p r o", o=1).to_broadcast([P, R4, F])

        def per_col(t):
            return t.rearrange("p (o n) -> p o n", o=1).to_broadcast([P, R4, F])

        def spare_column(e):
            return (spare[:, e, i:i + 1] for i in itertools.cycle(range(SPARES)))

        def settle(carrier, s, value):
            eng, carry = carrier
            eng.wait_ge(s, value)
            if not isinstance(value, int):
                carry()

        def blocks_loop(eng, body):
            body(0, True)
            with eng.Fori(1, BLOCKS // 2) as q:
                body(q, False)

        @block.sync
        def _(sp):
            sp.dma_start(X[:, :, :], x_d.rearrange("(t p) f -> p t f", p=P)).then_inc(x_in, 16)

            def load(s, c):
                sp.dma_start(quarter[c], adj_d[bass.ds(s * ROWS, ROWS), c * QCOLS:(c + 1) * QCOLS]
                             .rearrange("(r p) m -> p r m", p=P)).then_inc(adj_in[c], 16)

            def load_pass(base, after):
                for c in range(QUARTERS):
                    after(c)
                    load(0, c)
                with sp.Fori(1, BLOCKS) as s:
                    for c in range(QUARTERS):
                        sp.wait_ge(turned, s * TILES + (base - TILES + QT * (c + 1)))
                        load(s, c)

            def summed_slot(s, c):
                sp.wait_ge(summed_act if c % 2 else summed, s * 2 + (c // 2 + 1))

            for c in range(QUARTERS):
                load(0, c)
            with sp.Fori(1, BLOCKS) as s:
                for c in range(QUARTERS):
                    summed_slot(s - 1, c)
                    load(s, c)
            load_pass(0, lambda c: summed_slot(BLOCKS - 1, c))
            for e in range(2):
                sp.wait_ge(turned, STEPS - TILES + QT * (e + 1))
                sp.dma_start(ring[:, e, :], adj_d[e * P:(e + 1) * P, :]).then_inc(adj_in[e], 16)
            with sp.Fori(1, TILES // 2) as u:
                for e in range(2):
                    sp.wait_ge(multiplied, u * 4 + (2 * e - 2))
                    sp.dma_start(ring[:, e, :], adj_d[bass.ds(u * (2 * P) + e * P, P), :]).then_inc(adj_in[e], 16)

            def after_layer1(c):
                if c < 2:
                    sp.wait_ge(multiplied, 2 * (TILES - 2 + c + 1))
                else:
                    sp.wait_ge(et_turned, ESTEPS - GROUPS * (4 - c))
            load_pass(STEPS, after_layer1)
            load_pass(2 * STEPS, lambda c: sp.wait_ge(turned, 2 * STEPS - TILES + QT * (c + 1)))
            out_v = out_d.rearrange("(t p) f -> p t f", p=P)
            for s in range(BLOCKS):
                sp.wait_ge(x_final, s + 1)
                sp.dma_start(out_v[:, s * R4:(s + 1) * R4, :], X[:, s * R4:(s + 1) * R4, :]).then_inc(stored, 16)
            sp.wait_ge(stored, 16 * BLOCKS)

        @block.tensor
        def _(pe):
            pe.wait_ge(ident, 2)
            pe.wait_ge(il_ready, 1)
            pe.wait_ge(consts_in, 16 * CONST_DMAS)
            for k in range(2):
                mm = pe.matmul(PP[:, 1, 2 * k:2 * k + 2], W1[:, k * F:(k + 1) * F], w23[:, :], start=True, stop=True)
            mm.then_inc(u_done, 1)
            pe.wait_ge(u_spread, 1)

            def attention_sums(q, first):
                for e in range(2):
                    s = q * 2 + e
                    pe.wait_ge(in2_in[e], q * 16 + 16)
                    for k in range(2):
                        if not first:
                            pe.wait_ge(in2_copied, s * 2 + (k - 3))
                        for r in range(R4):
                            mm = pe.transpose(TP[2 * e + k][:, r * P:(r + 1) * P], in2[:, e, r, k * P:(k + 1) * P],
                                              idf[:, :])
                        mm.then_inc(in2_turned, 1)
                    pe.wait_ge(in2_copied, s * 2 + 2)
                    if not first:
                        pe.wait_ge(f_copied, s * 2 - 2)
                    for k in range(2):
                        pe.matmul(OT[e][:, :], u3B[:, k, :], in2T[:, e, k, :], start=(k == 0), stop=(k == 1))
                    for r in range(R4):
                        for k in range(2):
                            mm = pe.matmul(PP[:, e, 16 + r:17 + r], in2T[:, e, k, r * P:(r + 1) * P],
                                           u23[:, k, 0:1], start=(k == 0), stop=(k == 1))
                    mm.then_inc(f_done, 1)

            blocks_loop(pe, attention_sums)

            def turn(p, s, j):
                c = j // QT
                if j % QT == 0:
                    pe.wait_ge(adj_in[c], s * 16 + 16 * (QUARTER_USES[p][c] + 1))
                for r in range(R4):
                    mm = pe.transpose(TP[j % BUFS][:, r * P:(r + 1) * P],
                                      quarter[c][:, r, (j % QT) * P:(j % QT + 1) * P], idf[:, :])
                mm.then_inc(turned, 1)

            def product(p, s, e, j, first_block):
                y_hi, y_lo = FEATURES[p]
                if first_block and j % R4 == 0:
                    pe.wait_ge(y_ready, p * BLOCKS + j // R4 + 1)
                if j == 0:
                    if p == 0 and first_block:
                        pe.wait_ge(f_copied, 2 * BLOCKS)
                    elif p == 1 and first_block:
                        pe.wait_ge(l1_taken, BLOCKS - 1 + e)
                    else:
                        pe.wait_ge(oT_ready, s + (p * BLOCKS - 1))
                pe.wait_ge(lo_done, s * TILES + (p * STEPS + j + 1))
                if p < 2 and j == TILES - 1:
                    pe.wait_ge(staged, s + (p * BLOCKS + 1))
                    for r in range(R4):
                        for part in (stage_hi, stage_lo):
                            pe.matmul(OT[e][:, r * P:(r + 1) * P], part[:, r, :], idr[:, :], start=False, stop=False,
                                      skip_group_check=True)
                a_hi, a_lo = hi[:, j % BUFS, :], lo[:, j % BUFS, :]
                pe.matmul(OT[e][:, :], y_hi[:, j, :], a_hi, start=(j == 0), stop=False)
                pe.matmul(OT[e][:, :], y_hi[:, j, :], a_lo, start=False, stop=False)
                pe.matmul(OT[e][:, :], y_lo[:, j, :], a_hi, start=False, stop=(j == TILES - 1)).then_inc(spent, 1)

            def weigh(p, s, e):
                pe.wait_ge(oT_ready, s + (p * BLOCKS + 1))
                if p == 0:
                    if isinstance(s, int) and s == 0:
                        pe.wait_ge(f_copied, 2 * BLOCKS)
                    else:
                        pe.wait_ge(scaled, s)
                else:
                    if not (p == 1 and isinstance(s, int) and s == 0):
                        pe.wait_ge(pq_ready, s + (p - 1) * BLOCKS)
                for r in range(R4):
                    if p < 2:
                        mm = pe.matmul(PP[:, 0, r * P:(r + 1) * P], oT[e][:, r * P:(r + 1) * P],
                                       (W0, W2)[p][:, :], start=True, stop=True)
                    else:
                        mm = pe.matmul(PQ[:, r, :], oT[e][:, r * P:(r + 1) * P], IL[:, :], start=True, stop=True)
                mm.then_inc(post_done, 1)

            def turn_h(s):
                pe.wait_ge(hw_ready, s + 1)
                for r in range(R4):
                    mm = pe.transpose(PP[:, 1, r * P:(r + 1) * P], hw[:, r, :], idf[:, :])
                mm.then_inc(hT_turned, 1)

            def embed_h(s):
                pe.wait_ge(hT_ready, s + 1)
                for r in range(R4):
                    mm = pe.matmul(PQ[:, r, :], hT[:, r * P:(r + 1) * P], EL[:, :], start=True, stop=True)
                mm.then_inc(pq_done, 1)

            def stages(p, block_of, j):
                s, e = block_of
                if j == WEIGH:
                    weigh(p, s, e)
                if p == 1 and j == TURN_H:
                    turn_h(s)
                if p == 1 and j == EMBED_H:
                    embed_h(s)

            def gcn_pass(p):
                def body(q, first):
                    for k in range(2 * TILES):
                        e, j = divmod(k, TILES)
                        turn(p, q * 2 + e, j)
                        if k >= LAG:
                            e2, j2 = divmod(k - LAG, TILES)
                            product(p, q * 2 + e2, e2, j2, first and e2 == 0)
                        elif not first:
                            product(p, q * 2 - 1, 1, TILES + k - LAG, False)
                        elif p == 2:
                            product(1, BLOCKS - 1, 1, TILES + k - LAG, False)
                        if first and e == 0:
                            if p == 2:
                                stages(1, (BLOCKS - 1, 1), j)
                        else:
                            stages(p, (q * 2 + (e - 1), 1 - e), j)

                blocks_loop(pe, body)
                if p != 1:
                    for j in range(TILES - LAG, TILES):
                        product(p, BLOCKS - 1, 1, j, False)
                    weigh(p, BLOCKS - 1, 1)

            pe.wait_ge(ident_r, 1)
            gcn_pass(0)

            def turn_e(t, i, g):
                if g % (GROUPS // 2) == 0:
                    pe.wait_ge(exp_done, t * 2 + (g // (GROUPS // 2) + 1))
                for k in range(R4):
                    mm = pe.transpose(TP[g % BUFS][:, k * P:(k + 1) * P],
                                      LG[i % 4][:, (g * R4 + k) * P:(g * R4 + k + 1) * P], idf[:, :])
                mm.then_inc(et_turned, 1)

            def product_e(t, s, i, g, first_tile, first):
                if first_tile:
                    pe.wait_ge(h_ready, g + 1)
                if i % R4 == 0 and g == 0:
                    if first:
                        pe.wait_ge(oT_ready, BLOCKS - 1 + i // R4)
                    else:
                        pe.wait_ge(l1_taken, s - 1)
                pe.wait_ge(et_copied, t * GROUPS + (g + 1))
                r = i % R4
                for k in range(R4):
                    mm = pe.matmul(OT[i // R4][:, r * P:(r + 1) * P], ET[:, g % BUFS, k, :], H[:, g * R4 + k, :],
                                   start=(g == 0 and k == 0), stop=(g == GROUPS - 1 and k == R4 - 1))
                mm.then_inc(et_used, 1)

            def attend(q, first):
                for i in range(2 * R4):
                    for g in range(GROUPS):
                        turn_e(q * 8 + i, i, g)
                        i2, g2 = (i, g - 2) if g >= 2 else (i - 1, g + GROUPS - 2)
                        if i2 >= 0:
                            product_e(q * 8 + i2, q * 2 + i2 // R4, i2, g2, first and i2 == 0, first)
                        elif not first:
                            product_e(q * 8 - 1, q * 2 - 1, 7, g2, False, False)

            blocks_loop(pe, attend)
            for g in range(GROUPS - 2, GROUPS):
                product_e(TILES - 1, BLOCKS - 1, 7, g, False, False)

            gcn_pass(1)
            gcn_pass(2)

        @block.scalar
        def _(act):
            act_spare = spare_column(0)
            act_carry = (act, lambda: act.activation(next(act_spare), nhalf[:, 0:1], ACT.Copy))
            for dst, src in ((W0, w0_d), (W2, wg2_d), (EL[:, 0:F], emb_d), (EL[:, F:2 * F], lay_d[0:F, :]),
                             (IL[:, F:2 * F], lay_d[F:2 * F, :]), (W1, w1_d),
                             (w23[:, 0:1], w2_d.rearrange("(n a) -> n a", a=1)),
                             (w23[:, 1:2], w3_d.rearrange("(n a) -> n a", a=1)),
                             (b0B, b0_d.rearrange("(a n) -> a n", a=1).to_broadcast([P, F])),
                             (eB, eb_d.rearrange("(a n) -> a n", a=1).to_broadcast([P, F])),
                             (lB, lb_d.rearrange("(a n) -> a n", a=1).to_broadcast([P, F])),
                             (b23[:, 0:1], b2_d.rearrange("(a n) -> a n", a=1).to_broadcast([P, 1])),
                             (b23[:, 1:2], b3_d.rearrange("(a n) -> a n", a=1).to_broadcast([P, 1]))):
                act.dma_start(dst[:, :], src).then_inc(consts_in, 16)
            act.dma_start(in2[:, 0, :, :], in2_d[0:ROWS, :].rearrange("(r p) m -> p r m", p=P)).then_inc(in2_in[0], 16)
            act.dma_start(in2[:, 1, :, :], in2_d[ROWS:2 * ROWS, :].rearrange("(r p) m -> p r m", p=P))\
               .then_inc(in2_in[1], 16)
            act.wait_ge(ident, 2)
            act.activation(idr[:, :], idf[:, :], ACT.Copy).then_inc(ident_r, 1)
            act.wait_ge(u_done, 1)
            act.activation(u23[:, :, :].rearrange("p a b -> p (a b)"), PP[:, 1, 0:4], ACT.Copy).then_inc(u_copied, 1)
            act.wait_ge(u_copied, 1)
            act.wait_ge(consts, 5)
            act.activation(u3B[:, 0, :], ones[:, :], ACT.Copy, scale=u23[:, 0, 1:2])
            act.activation(u3B[:, 1, :], ones[:, :], ACT.Copy, scale=u23[:, 1, 1:2]).then_inc(u_spread, 1)
            act.wait_ge(consts_in, 16 * CONST_DMAS)
            act.activation(sink[:, 0, :], eB[:, :], ACT.Square, accum_out=y2[:, 0:1]).then_inc(y2_done, 1)
            act.wait_ge(y2_done, 1)
            act.activation(sink[:, 1, :], lB[:, :], ACT.Square, accum_out=y2[:, 1:2]).then_inc(y2_done, 1)

            def row_sums(s, c, first):
                if c == 1 and not first:
                    settle(act_carry, deg_ready, s)
                act.wait_ge(adj_in[c], s * 16 + 16)
                for r in range(R4):
                    ins = act.activation(quarter[c][:, r, :], quarter[c][:, r, :], ACT.Copy,
                                         accum_out=dpart[:, c, r:r + 1])
                ins.then_inc(summed_act, 1)

            def attention_sums(q, first):
                for e in range(2):
                    s = q * 2 + e
                    row_sums(s, 1, first and e == 0)
                    for k in range(2):
                        act.wait_ge(in2_turned, s * 2 + (k + 1))
                        act.activation(in2T[:, e, k, :], TP[2 * e + k][:, :], ACT.Copy).then_inc(in2_copied, 1)
                    settle(act_carry, f_done, s + 1)
                    act.activation(f2B[:, bass.ds(s * ROWS, ROWS)], OT[e][:, :], ACT.Identity, bias=b23[:, 1:2])\
                       .then_inc(f_copied, 1)
                    act.activation(cols_of(f1, s), PP[:, e, 16:20], ACT.Identity, bias=b23[:, 0:1])\
                       .then_inc(f_copied, 1)
                    row_sums(s, 3, False)

            def load_in2(s, e):
                act.dma_start(in2[:, e, :, :], in2_d[bass.ds(s * ROWS, ROWS), :].rearrange("(r p) m -> p r m", p=P))\
                   .then_inc(in2_in[e], 16)

            attention_sums(0, True)
            with act.Fori(1, BLOCKS // 2) as q:
                for e in range(2):
                    load_in2(q * 2 + e, e)
                attention_sums(q, False)

            def split_hi(p, s, j, first):
                act.wait_ge(turned, s * TILES + (p * STEPS + j + 1))
                if first and j < BUFS:
                    if p == 0:
                        act.wait_ge(f_done, BLOCKS)
                    elif p == 1:
                        act.wait_ge(et_used, ESTEPS)
                    else:
                        act.wait_ge(spent, p * STEPS + j - BUFS + 1)
                else:
                    act.wait_ge(spent, s * TILES + (p * STEPS + j - BUFS + 1))
                act.activation(hi[:, j % BUFS, :], TP[j % BUFS][:, :], ACT.Copy).then_inc(hi_done, 1)

            def take_sums(p, s, e):
                act.wait_ge(spent, s * TILES + (p * STEPS + TILES))
                act.activation(oT[e][:, :], OT[e][:, :], ACT.Copy).then_inc(oT_ready, 1)

            def squares(src, dst, ready, part=None):
                for r in range(R4) if part is None else (2 * part, 2 * part + 1):
                    ins = act.activation(sink[:, r, :], src[:, r, 0:F], ACT.Square, accum_out=dst[:, r:r + 1])
                if part != 0:
                    ins.then_inc(ready, 1)

            def take_hT(s):
                act.wait_ge(hT_turned, s + 1)
                act.activation(hT, PP[:, 1, :], ACT.Copy).then_inc(hT_ready, 1)

            def take_pq(p, s):
                if p == 1:
                    act.wait_ge(pq_done, s + 1)
                else:
                    act.wait_ge(post_done, s + (2 * BLOCKS + 1))
                if not (p == 1 and isinstance(s, int) and s == 0):
                    act.wait_ge(pq_used, s + (p - 1) * BLOCKS)
                    if p == 1:
                        act.wait_ge(q_kept, s)
                    else:
                        act.wait_ge(q_kept, BLOCKS)
                act.activation(pq[:, :, :], PQ[:, :, :], ACT.Copy).then_inc(pq_ready, 1)

            def logs(n):
                act.wait_ge(nrm_ready, n)
                act.activation(ln1[:, :], nrc[:, :], ACT.Ln, bias=1.0)
                act.activation(ln2[:, :], nrc[:, :], ACT.Ln, bias=1.0, scale=-1.0).then_inc(ln_ready, 1)

            def tanh(n):
                act.wait_ge(nth_ready, n)
                act.activation(th[:, :], nth[:, :], ACT.Tanh).then_inc(th_ready, 1)

            L2_LOGS, L2_TANHS = 2 * BLOCKS, BLOCKS

            def post2(s, j):
                if j == TURN_H - 1:
                    act.wait_ge(hw_ready, s + 1)
                    squares(hw, sq1, sq1_ready, 0)
                if j == TURN_H:
                    squares(hw, sq1, sq1_ready, 1)
                if j == TURN_H + 1:
                    take_hT(s)
                if j == TAKE_PQ2:
                    take_pq(1, s)
                if j == TAKE_PQ2 + 1:
                    act.wait_ge(pq_ready, s + 1)
                    squares(pq, sq2, sq2_ready, 0)
                if j == TAKE_PQ2 + 2:
                    squares(pq, sq2, sq2_ready, 1)
                if j == LOGS2:
                    logs(s * 2 + 1)
                if j == TANH2:
                    tanh(s + 1)
                if j == MOBIUS2 + 3:
                    act.wait_ge(mixed, s + 1)
                    squares(hv, sq3, sq3_ready, 0)
                if j == MOBIUS2 + 4:
                    squares(hv, sq3, sq3_ready, 1)
                if j == LOGS2B:
                    logs(s * 2 + 2)

            def post3(s, j):
                if j == TAKE_PQ3:
                    take_pq(2, s)
                if j == TAKE_PQ3 + 1:
                    act.wait_ge(pq_ready, s + (BLOCKS + 1))
                    squares(pq, sq1, sq1_ready, 0)
                if j == TAKE_PQ3 + 2:
                    squares(pq, sq1, sq1_ready, 1)
                if j == TANH3:
                    tanh(s * 2 + (L2_TANHS + 1))
                if j == LOGS3:
                    logs(s + (L2_LOGS + 1))
                if j == W3 + 3:
                    act.wait_ge(w_ready, s + 1)
                    squares(hv, sq2, sq2_ready, 0)
                if j == W3 + 4:
                    squares(hv, sq2, sq2_ready, 1)
                if j == TANH3B:
                    tanh(s * 2 + (L2_TANHS + 2))

            def gcn_pass(p):
                def stages(p, s, e, j):
                    if j == TAKE_SUMS:
                        take_sums(p, s, e)
                    (lambda s, j: None, post2, post3)[p](s, j)

                def body(q, first):
                    for k in range(2 * TILES):
                        e, j = divmod(k, TILES)
                        split_hi(p, q * 2 + e, j, first and e == 0)
                        if not first:
                            stages(p, q * 2 + (e - 2), e, TILES + j)
                        if not (first and e == 0):
                            stages(p, q * 2 + (e - 1), 1 - e, j)
                        elif p == 2:
                            stages(1, BLOCKS - 2, 0, TILES + j)
                            stages(1, BLOCKS - 1, 1, j)
                        if p == 2 and first and k == TILES - 1:
                            for late in range(TILES, 2 * TILES):
                                stages(1, BLOCKS - 1, 1, late)

                blocks_loop(act, body)
                if p == 0:
                    take_sums(p, BLOCKS - 1, 1)
                if p == 2:
                    for j in range(2 * TILES):
                        if j < TILES:
                            stages(p, BLOCKS - 2, 0, TILES + j)
                        stages(p, BLOCKS - 1, 1, j)

            def bend(t, i, c):
                half_of = slice(c * HALF, (c + 1) * HALF)
                act.activation(LG[i % 4][:, half_of], f2B[:, half_of], ACT.Relu, bias=mf1[:, bass.ds(t, 1)],
                               scale=SLOPE - 1.0).then_inc(bent, 1)

            act.wait_ge(mf1_ready, 1)
            act.wait_ge(f_copied, 2 * BLOCKS)
            for c in range(2):
                bend(0, 0, c)
            gcn_pass(0)

            def exps(t, i, c):
                lg = LG[i % 4][:, c * HALF:(c + 1) * HALF]
                act.wait_ge(m_ready, t + 1)
                act.activation(lg, lg, ACT.Exp, bias=negm[:, i % 4:i % 4 + 1],
                               accum_out=rsum[:, i // R4, c, i % R4:i % R4 + 1]).then_inc(exp_done, 1)

            def take_e(t, g, first_tile):
                act.wait_ge(et_turned, t * GROUPS + (g + 1))
                if first_tile and g < BUFS:
                    act.wait_ge(spent, STEPS)
                else:
                    act.wait_ge(et_used, t * GROUPS + (g - BUFS + 1))
                act.activation(ET[:, g % BUFS, :, :].rearrange("p k m -> p (k m)"), TP[g % BUFS][:, :], ACT.Copy)\
                   .then_inc(et_copied, 1)

            def beside(t, i, first_tile, parts):
                for g in range(GROUPS):
                    if g % 2 == 0:
                        parts[g // 2]()
                    take_e(t, g, first_tile)

            def attend(q, first):
                for i in range(2 * R4):
                    t = q * 8 + i

                    def bend_part(c):
                        if not first:
                            settle(act_carry, et_turned, t * GROUPS + ((c + 1) * (GROUPS // 2) - 4 * GROUPS))
                        elif i == 3:
                            act.wait_ge(post_done, BLOCKS)
                        elif i > 3:
                            act.wait_ge(et_turned, (i - 4) * GROUPS + (c + 1) * (GROUPS // 2))
                        elif i:
                            act.wait_ge(turned, STEPS)
                        bend(t, i, c)

                    if first and i < 3:
                        for c in range(2):
                            if i:
                                bend_part(c)
                    elif first and i == 3:
                        for c in range(2):
                            exps(0, 0, c)
                            bend_part(c)
                    else:
                        j = (i - 3) % 8
                        beside(t - 4, (i - 4) % 8, first and i == 4,
                               (lambda: exps(t - 3, j, 0), lambda: exps(t - 3, j, 1),
                                lambda: bend_part(0), lambda: bend_part(1)))

            blocks_loop(act, attend)
            for t in range(TILES - 3, TILES):
                beside(t - 1, (t - 1) % 8, False,
                       (lambda: exps(t, t % 8, 0), lambda: exps(t, t % 8, 1), lambda: None, lambda: None))
            for g in range(GROUPS):
                take_e(TILES - 1, g, False)

            gcn_pass(1)
            gcn_pass(2)

        @block.vector
        def _(dve):
            dve_spare = spare_column(1)
            dve_carry = (dve, lambda: dve.memset(next(dve_spare), 0.0))

            def ln_sums(prep, s, part):
                if part == 0:
                    dve.wait_ge(x_new, s + (prep * BLOCKS + 1))
                for r in (2 * part, 2 * part + 1):
                    ins = dve.bn_stats(st[:, r, :], xw[:, r, :])
                if part:
                    ins.then_inc(bn_stat, 1)

            def ln_variance(prep, s):
                n = s + (prep * BLOCKS + 1)
                settle(dve_carry, bn_stat, n)
                for r in range(R4):
                    ins = dve.bn_aggr(mv[:, r, :], st[:, r, :])
                ins.then_inc(bn_agg, 1)
                dve.wait_ge(bn_agg, n)
                dve.tensor_scalar(ve[:, :], mv[:, :, 1], LN_EPS, None, ALU.add).then_inc(var_ready, 1)

            def ln_scale(prep, s, part):
                if part == 0:
                    dve.wait_ge(rstd_ready, s + (prep * BLOCKS + 1))
                for r in (2 * part, 2 * part + 1):
                    ins = dve.tensor_scalar(yw[:, r, :], xw[:, r, :], mv[:, r, 0:1], rs[:, r:r + 1],
                                            ALU.subtract, ALU.mult)
                if part:
                    ins.then_inc(normed, 1)

            def ln_relu(prep, s):
                dve.wait_ge(normed, s + (prep * BLOCKS + 1))
                if prep == 1:
                    dve.tensor_scalar(tiles_of(H, s), yw[:, :, :], 0.0, None, ALU.max).then_inc(h_ready, 1)
                elif prep == 3:
                    dve.tensor_scalar(hw[:, :, :], yw[:, :, :], 0.0, None, ALU.max).then_inc(hw_ready, 1)
                else:
                    dve.tensor_scalar(tiles_of(YA[0], s), yw[:, :, :], 0.0, None, ALU.max).then_inc(yhi_ready, 1)

            def ln_lo(prep, s):
                dve.wait_ge(yhi_ready, s + (prep // 2 * BLOCKS + 1))
                dve.scalar_tensor_tensor(out=tiles_of(YA[1], s), in0=yw[:, :, :], scalar=0.0,
                                         in1=tiles_of(YA[0], s).bitcast(F32), op0=ALU.max, op1=ALU.subtract)\
                   .then_inc(y_ready, 1)

            def keep_x(prep, s):
                dve.tensor_scalar(tiles_of(X, s), xw[:, :, :], 1.0, None, ALU.mult).then_inc(x_kept, 1)

            def stage(p, s):
                if not (p == 0 and isinstance(s, int) and s == 0):
                    dve.wait_ge(spent, s * TILES + p * STEPS)
                dve.tensor_scalar(stage_hi[:, :, :], tiles_of(YA[0], s).bitcast(F32), 1.0, None, ALU.mult)
                dve.tensor_scalar(stage_lo[:, :, :], tiles_of(YA[1], s).bitcast(F32), 1.0, None, ALU.mult)\
                   .then_inc(staged, 1)

            dve.wait_ge(x_in, 16)

            def scale_features0(s):
                for part in range(2):
                    ln_scale(0, s, part)
                ln_relu(0, s)
                ln_lo(0, s)

            def degrees(q, first):
                for e in range(2):
                    s = q * 2 + e
                    if not (first and e == 0):
                        settle(dve_carry, deg_ready, s)
                    dve.wait_ge(adj_in[0], s * 16 + 16)
                    dve.tensor_reduce(dpart[:, 0, :], quarter[0], AX.X, ALU.add).then_inc(summed, 1)
                    if not (first and e == 0):
                        scale_features0(s - 1)
                        dve.wait_ge(y_ready, s)
                    dve.tensor_copy(xw[:, :, :], tiles_of(X, s)).then_inc(x_new, 1)
                    ln_sums(0, s, 0)
                    ln_sums(0, s, 1)
                    ln_variance(0, s)
                    dve.wait_ge(adj_in[2], s * 16 + 16)
                    dve.tensor_reduce(dpart[:, 2, :], quarter[2], AX.X, ALU.add).then_inc(summed, 1)
                    settle(dve_carry, summed_act, s * 2 + 2)
                    settle(dve_carry, summed, s * 2 + 2)
                    dve.tensor_reduce(cols_of(deg, s), dpart[:, :, :].rearrange("p c r -> p r c"), AX.X, ALU.add)\
                       .then_inc(deg_ready, 1)

            blocks_loop(dve, degrees)
            scale_features0(BLOCKS - 1)
            dve.wait_ge(f_copied, 2 * BLOCKS)
            dve.tensor_scalar(mf1[:, :], f1[:, :], SLOPE - 1.0, None, ALU.mult).then_inc(mf1_ready, 1)
            dve.wait_ge(d_ready, 2)

            def split_lo(p, s, j):
                dve.wait_ge(hi_done, s * TILES + (p * STEPS + j + 1))
                dve.tensor_tensor(lo[:, j % BUFS, :], TP[j % BUFS][:, :], hi[:, j % BUFS, :].bitcast(F32),
                                  ALU.subtract).then_inc(lo_done, 1)

            def xw_free(prep, s):
                if not (prep == 1 and isinstance(s, int) and s == 0):
                    dve.wait_ge(x_kept, s + (prep - 1) * BLOCKS)

            def post0(s, j):
                if j == WEIGH + 2:
                    dve.wait_ge(post_done, s + 1)
                    if isinstance(s, int) and s == 0:
                        dve.wait_ge(y_ready, BLOCKS)
                    else:
                        dve.wait_ge(h_ready, s)
                    dve.tensor_tensor(yw[:, :, :], PP[:, 0, :].rearrange("p (r n) -> p r n", r=R4),
                                      per_row(cols_of(d0, s)), ALU.mult).then_inc(scaled, 1)
                if j == WEIGH + 3:
                    dve.wait_ge(scaled, s + 1)
                    dve.tensor_tensor(yw[:, :, :], yw[:, :, :], per_col(b0B[:, :]), ALU.add).then_inc(biased0, 1)
                if j == WEIGH + 4:
                    dve.wait_ge(biased0, s + 1)
                    xw_free(1, s)
                    dve.scalar_tensor_tensor(out=xw[:, :, :], in0=yw[:, :, :], scalar=0.0, in1=tiles_of(X, s),
                                             op0=ALU.max, op1=ALU.add).then_inc(x_new, 1)
                norm_steps(1, s, j - (WEIGH + 5))

            def norm_steps(prep, s, j):
                if j in (0, 1):
                    ln_sums(prep, s, j)
                if j == 2:
                    ln_variance(prep, s)
                if j == 3:
                    keep_x(prep, s)
                if j in (5, 6):
                    ln_scale(prep, s, j - 5)
                if j == 7:
                    ln_relu(prep, s)
                if j == 8 and prep == 2:
                    ln_lo(prep, s)

            def post2(s, j):
                if j == WEIGH + 2:
                    dve.wait_ge(post_done, s + (BLOCKS + 1))
                    dve.scalar_tensor_tensor(out=yw[:, :, :], in0=PP[:, 0, :].rearrange("p (r n) -> p r n", r=R4),
                                             scalar=0.0, in1=per_row(cols_of(d2, s)), op0=ALU.max, op1=ALU.mult)\
                       .then_inc(scaled, 1)
                if j == WEIGH + 3:
                    dve.wait_ge(scaled, s + (BLOCKS + 1))
                    xw_free(3, s)
                    dve.tensor_tensor(xw[:, :, :], yw[:, :, :], tiles_of(X, s), ALU.add).then_inc(x_new, 1)
                norm_steps(3, s, j - (WEIGH + 4))
                if j in (DOT2, DOT2 + 1):
                    bias_dot(pq, eB, pq_ready, s + 1, j - DOT2)
                if j == DOT2 + 2:
                    dve.wait_ge(sq1_ready, s + 1)
                    dve.tensor_scalar(tiles_of(H, s), pq[:, :, F:2 * F], 1.0, None, ALU.mult).then_inc(q_kept, 1)
                    dve.tensor_scalar(cols_of(nh2, s), sq1[:, :], 1.0, None, ALU.mult).then_inc(nh2_kept, 1)
                mobius(pq[:, :, 0:F], eB, s, s + 1, pq_used, j - MOBIUS2)
                late2(s, j - LATE2)

            def bias_dot(src, bias, ready, n, part):
                if part == 0:
                    dve.wait_ge(ready, n)
                for r in (2 * part, 2 * part + 1):
                    ins = dve.tensor_tensor_reduce(sink2[:, r, :], src[:, r, 0:F], bias[:, :], 1.0, 0.0, ALU.mult,
                                                   ALU.add, dot[:, r:r + 1])
                if part:
                    ins.then_inc(dot_ready, 1)

            def mobius(src, bias, s, n, used, j):
                dst = hv if used is not None else yw
                if j == 0:
                    dve.wait_ge(mix_ready, n)
                    dve.tensor_tensor(dst[:, :, :], src, per_row(al[:, :]), ALU.mult)\
                       .then_inc(used if used is not None else w_scaled, 1)
                if j == 1:
                    dve.tensor_tensor(tw[:, :, :], per_col(bias[:, :]), per_row(be[:, :]), ALU.mult)\
                       .then_inc(bias_scaled, 1)
                if j == 2:
                    dve.wait_ge(bias_scaled, n)
                    dve.tensor_tensor(dst[:, :, :], dst[:, :, :], tw[:, :, :], ALU.add).then_inc(mixed, 1)

            def late2(s, j):
                if j == 0:
                    dve.wait_ge(s_ready, s + 1)
                    dve.tensor_tensor(tw[:, :, :], hv[:, :, :], per_row(sc1[:, :]), ALU.mult).then_inc(y3_scaled, 1)
                if j == 1:
                    dve.wait_ge(y3_scaled, s + 1)
                    dve.tensor_scalar(tiles_of(YB[0], s), tw[:, :, :], 1.0, None, ALU.mult).then_inc(yhi_ready, 1)
                if j == 2:
                    dve.wait_ge(yhi_ready, s + (2 * BLOCKS + 1))
                    dve.tensor_tensor(tiles_of(YB[1], s), tw[:, :, :], tiles_of(YB[0], s).bitcast(F32),
                                      ALU.subtract).then_inc(y_ready, 1)

            def post3(s, j):
                if j == W3:
                    dve.wait_ge(coef_ready, s + 1)
                    dve.tensor_tensor(hv[:, :, :], tiles_of(H, s), per_row(sc0[:, :]), ALU.mult)
                if j == W3 + 1:
                    dve.tensor_tensor(tw[:, :, :], pq[:, :, F:2 * F], per_row(sc1[:, :]), ALU.mult)\
                       .then_inc(pq_used, 1)
                if j == W3 + 2:
                    dve.wait_ge(pq_used, s + (BLOCKS + 1))
                    dve.tensor_tensor(hv[:, :, :], hv[:, :, :], tw[:, :, :], ALU.add).then_inc(w_ready, 1)
                if j in (W3 + 4, W3 + 5):
                    bias_dot(hv, lB, w_ready, s + 1, j - (W3 + 4))
                mobius(hv[:, :, :], lB, s, s + (BLOCKS + 1), None, j - MOBIUS3)
                if j == MOBIUS3 + 3:
                    dve.wait_ge(mixed, s + (BLOCKS + 1))
                    dve.tensor_tensor(tiles_of(X, s), yw[:, :, :], tiles_of(X, s), ALU.add).then_inc(x_final, 1)

            def gcn_pass(p):
                post = (post0, post2, post3)[p]

                def body(q, first):
                    for k in range(2 * TILES):
                        e, j = divmod(k, TILES)
                        split_lo(p, q * 2 + e, j)
                        if p < 2 and j == STAGE:
                            stage(p, q * 2 + e)
                        if not first:
                            post(q * 2 + (e - 2), TILES + j)
                        if not (first and e == 0):
                            post(q * 2 + (e - 1), j)
                        elif p == 1:
                            take_attention(BLOCKS - 1, 1, j - 4)
                        elif p == 2:
                            post2(BLOCKS - 2, TILES + j)
                            post2(BLOCKS - 1, j)
                        if p == 2 and first and k == TILES - 1:
                            for late in range(TILES, 2 * TILES):
                                post2(BLOCKS - 1, late)

                blocks_loop(dve, body)
                if p == 2:
                    for j in range(2 * TILES):
                        if j < TILES:
                            post3(BLOCKS - 2, TILES + j)
                        post3(BLOCKS - 1, j)

            gcn_pass(0)
            for j in range(WEIGH + 8):
                post0(BLOCKS - 1, j)

            def logits(t, i):
                a, lg = ring[:, i % 2, :], LG[i % 4]
                dve.wait_ge(adj_in[i % 2], (t - i % 2) * 8 + 16 * (ROWTILE_USES + 1))
                for c in range(2):
                    n = t * 2 + (c + 1)
                    half_of = slice(c * HALF, (c + 1) * HALF)
                    if isinstance(n, int) and n == 1:
                        dve.wait_ge(spent, STEPS)
                    else:
                        dve.wait_ge(masked, n - 1)
                    dve.tensor_scalar(R[:, :], a[:, half_of], 0.0, MASKED, ALU.is_le, ALU.mult).then_inc(biased, 1)
                    settle(dve_carry, bent_added, n)
                    dve.scalar_tensor_tensor(out=lg[:, half_of], in0=lg[:, half_of], scalar=f1[:, bass.ds(t, 1)],
                                             in1=a[:, half_of], op0=ALU.add, op1=ALU.mult).then_inc(multiplied, 1)
                    settle(dve_carry, biased, n)
                    settle(dve_carry, multiplied, n)
                    dve.tensor_tensor_reduce(lg[:, half_of], lg[:, half_of], R[:, :], 1.0,
                                             -3e38 if c == 0 else mx[:, 0:1], ALU.add, ALU.max, mx[:, c:c + 1])\
                       .then_inc(masked, 1)
                dve.wait_ge(masked, t * 2 + 2)
                dve.tensor_scalar(negm[:, i % 4:i % 4 + 1], mx[:, 1:2], -1.0, None, ALU.mult).then_inc(m_ready, 1)

            def take_attention(s, e, j):
                if j == 0:
                    dve.wait_ge(et_used, (s * R4 + R4) * GROUPS)
                    dve.tensor_tensor(rcp[:, :], rsum[:, e, 0, :], rsum[:, e, 1, :], ALU.add).then_inc(rsum_added, 1)
                    dve.wait_ge(rsum_added, s + 1)
                    dve.reciprocal(rcp[:, :], rcp[:, :]).then_inc(rcp_ready, 1)
                    dve.wait_ge(rcp_ready, s + 1)
                    dve.tensor_tensor(yw[:, :, :], OT[e][:, :].rearrange("p (r n) -> p r n", r=R4),
                                      per_row(rcp[:, :]), ALU.mult).then_inc(l1_taken, 1)
                if j == 1:
                    dve.wait_ge(l1_taken, s + 1)
                    xw_free(2, s)
                    dve.tensor_tensor(xw[:, :, :], yw[:, :, :], tiles_of(X, s), ALU.add).then_inc(x_new, 1)
                norm_steps(2, s, j - 2)

            def attend(q, first):
                for i in range(2 * R4):
                    t = q * 8 + i
                    logits(t, i)
                    if first and i == 0:
                        for j in range(WEIGH + 8, TILES):
                            post0(BLOCKS - 1, j)
                    if not first and i in (2, 3):
                        for j in (range(0, 6), range(6, 12))[i - 2]:
                            take_attention(q * 2 - 1, 1, j)
                    if i in (6, 7):
                        for j in (range(0, 6), range(6, 12))[i - 6]:
                            take_attention(q * 2, 0, j)

            blocks_loop(dve, attend)

            gcn_pass(1)
            gcn_pass(2)

        @block.gpsimd
        def _(pool):
            pool_spare = spare_column(2)

            def idle():
                return pool.tensor_tensor(next(pool_spare), half[:, 0:1], half[:, 0:1], ALU.add)

            pool_carry = (pool, idle)
            pool.memset(idf[:, :], 0.0).then_inc(ident, 1)
            pool.memset(ones[:, :], 1.0).then_inc(consts, 1)
            pool.memset(nhalf[:, :], -0.5).then_inc(consts, 1)
            pool.memset(half[:, :], 0.5).then_inc(consts, 1)
            pool.memset(mone[:, :], -1.0).then_inc(consts, 1)
            pool.memset(one[:, :], 1.0).then_inc(consts, 1)
            pool.wait_ge(ident, 1)
            pool.affine_select(out=idf[:, :], in_=idf[:, :], compare_op=ALU.not_equal, fill=1.0, base=0,
                               pattern=[[-1, P]], channel_multiplier=1).then_inc(ident, 1)
            pool.wait_ge(ident, 2)
            pool.wait_ge(consts, 5)
            pool.tensor_copy(IL[:, 0:F], idf[:, :]).then_inc(il_ready, 1)

            def root(prep, s):
                n = s + (prep * BLOCKS + 1)
                pool.wait_ge(var_ready, n)
                if prep != 2:
                    pool.tensor_tensor(rs[:, :], ve[:, :], nhalf[:, 0:R4], ALU.pow).then_inc(rstd_ready, 1)
                else:
                    pool.tensor_tensor(ps[:, 0, :], ve[:, :], nhalf[:, 0:R4], ALU.pow).then_inc(pow_done, 1)
                    settle(pool_carry, pow_done, s + 1)
                    pool.tensor_tensor(rs[:, :], ps[:, 0, :], cols_of(d2, s), ALU.mult).then_inc(rstd_ready, 1)

            with pool.Fori(0, BLOCKS) as s:
                pool.wait_ge(var_ready, s + 1)
                pool.tensor_tensor(ps[:, 0, :], ve[:, :], nhalf[:, 0:R4], ALU.pow)
                settle(pool_carry, deg_ready, s + 1)
                pool.tensor_tensor(ps[:, 1, :], cols_of(deg, s), one[:, :], ALU.add).then_inc(d_step, 1)
                settle(pool_carry, d_step, s * 2 + 1)
                pool.tensor_tensor(cols_of(d0, s), ps[:, 1, :], nhalf[:, 0:R4], ALU.pow).then_inc(d_step, 1)
                settle(pool_carry, d_step, s * 2 + 2)
                pool.tensor_tensor(rs[:, :], ps[:, 0, :], cols_of(d0, s), ALU.mult).then_inc(rstd_ready, 1)
            pool.tensor_scalar(deg[:, :], deg[:, :], 1.0, None, ALU.add).then_inc(d_ready, 1)
            pool.wait_ge(d_ready, 1)
            pool.tensor_scalar(deg2[:, :], deg[:, :], DEG_EPS, None, ALU.add).then_inc(d_step, 1)
            pool.wait_ge(d_step, 2 * BLOCKS + 1)
            pool.tensor_tensor(d2[:, :], deg2[:, :], nhalf[:, :], ALU.pow).then_inc(d_ready, 1)
            pool.wait_ge(d_ready, 2)

            def add_f2(t, i):
                for c in range(2):
                    half_of = slice(c * HALF, (c + 1) * HALF)
                    pool.wait_ge(bent, t * 2 + (c + 1))
                    pool.tensor_tensor(LG[i % 4][:, half_of], LG[i % 4][:, half_of], f2B[:, half_of], ALU.add)\
                        .then_inc(bent_added, 1)

            add_f2(0, 0)
            with pool.Fori(0, BLOCKS) as s:
                root(1, s)
            for t in range(1, 2 * R4):
                add_f2(t, t)
            root(2, 0)
            with pool.Fori(1, BLOCKS - 1) as s:
                for i in range(R4, 2 * R4):
                    add_f2(s * R4 + i, i)
                root(2, s)
            root(2, BLOCKS - 1)

            class Chain:

                def __init__(self, base):
                    self.base, self.n = base, 0

                def then(self, ins):
                    ins.then_inc(pool_step, 1)
                    self.n += 1
                    pool.wait_ge(pool_step, self.base + self.n)

                def tt(self, out, a, b, op):
                    self.then(pool.tensor_tensor(out, a, b, op))

                def ts(self, out, a, s1, s2, op0, op1=ALU.bypass):
                    idle()
                    self.then(pool.tensor_scalar(out, a, s1, s2, op0, op1) if s2 is not None
                              else pool.tensor_scalar(out, a, s1, None, op0))

            def bounded_norm(ch, out, square, scale=None):
                ch.tt(out, square, half[:, :], ALU.pow)
                if scale is not None:
                    ch.tt(out, out, scale, ALU.mult)
                ch.ts(out, out, H_EPS, None, ALU.max)

            def log_map(ch, out, n_logs):
                ch.ts(nrc[:, :], nrm[:, :], MAX_TANH, None, ALU.min)
                idle().then_inc(nrm_ready, 1)
                t, p, m, c = (ps[:, i, :] for i in range(4))
                ch.tt(t, nrc[:, :], nrc[:, :], ALU.mult)
                ch.ts(p, t, 1.0 / 9, 1.0 / 7, ALU.mult, ALU.add)
                for k in (1.0 / 5, 1.0 / 3, 1.0):
                    ch.tt(p, p, t, ALU.mult)
                    ch.ts(p, p, k, None, ALU.add)
                ch.ts(m, t, 1.0 / 64, None, ALU.is_lt)
                ch.tt(c, nrc[:, :], mone[:, :], ALU.pow)
                ch.tt(out, nrm[:, :], mone[:, :], ALU.pow)
                ch.tt(out, out, nrc[:, :], ALU.mult)
                pool.wait_ge(ln_ready, n_logs)
                lg = ps[:, 4, :]
                ch.tt(lg, ln1[:, :], ln2[:, :], ALU.subtract)
                ch.tt(lg, lg, half[:, :], ALU.mult)
                ch.tt(lg, lg, c, ALU.mult)
                ch.tt(p, p, lg, ALU.subtract)
                ch.tt(p, p, m, ALU.mult)
                ch.tt(p, p, lg, ALU.add)
                ch.tt(out, out, p, ALU.mult)

            def mix(ch, square, y2c, scale, n_sq, n_dot, n_tanhs):
                pool.wait_ge(sq2_ready, n_sq)
                pool.wait_ge(dot_ready, n_dot)
                bounded_norm(ch, nth[:, :], square, scale)
                idle().then_inc(nth_ready, 1)
                g, xy, x2, a, d = (ps[:, i, :] for i in range(5))
                ch.tt(g, nth[:, :], mone[:, :], ALU.pow)
                if scale is not None:
                    ch.tt(g, g, scale, ALU.mult)
                pool.wait_ge(th_ready, n_tanhs)
                ch.tt(g, g, th[:, :], ALU.mult)
                ch.tt(xy, g, dot[:, :], ALU.mult)
                ch.tt(x2, g, g, ALU.mult)
                ch.tt(x2, x2, square, ALU.mult)
                ch.ts(xy, xy, 2.0, 1.0, ALU.mult, ALU.add)
                yy = y2c.to_broadcast([P, R4])
                ch.tt(a, xy, yy, ALU.add)
                ch.tt(d, x2, yy, ALU.mult)
                ch.tt(d, d, xy, ALU.add)
                ch.ts(d, d, H_EPS, None, ALU.max)
                ch.tt(d, d, mone[:, :], ALU.pow)
                ch.tt(a, a, g, ALU.mult)
                ch.tt(al[:, :], a, d, ALU.mult)
                ch.ts(x2, x2, -1.0, 1.0, ALU.mult, ALU.add)
                ch.tt(be[:, :], x2, d, ALU.mult)
                idle().then_inc(mix_ready, 1)

            def post2(s):
                root(3, s)
                settle(pool_carry, sq1_ready, s + 1)
                ch = Chain(s * PER2)
                bounded_norm(ch, nrm[:, :], sq1[:, :])
                log_map(ch, sc0[:, :], s * 2 + 1)
                mix(ch, sq2[:, :], y2[:, 0:1], sc0[:, :], s + 1, s + 1, s + 1)
                settle(pool_carry, sq3_ready, s + 1)
                bounded_norm(ch, nrm[:, :], sq3[:, :])
                log_map(ch, sc1[:, :], s * 2 + 2)
                idle().then_inc(s_ready, 1)
                assert ch.n == PER2, ch.n

            def post3(s):
                settle(pool_carry, sq1_ready, s + (BLOCKS + 1))
                ch = Chain(s * PER3 + PER2 * BLOCKS)
                bounded_norm(ch, nth[:, :], sq1[:, :])
                idle().then_inc(nth_ready, 1)
                g, n2 = ps[:, 5, :], ps[:, 6, :]
                ch.tt(g, nth[:, :], mone[:, :], ALU.pow)
                pool.wait_ge(th_ready, s * 2 + (BLOCKS + 1))
                ch.tt(g, g, th[:, :], ALU.mult)
                ch.tt(n2, g, g, ALU.mult)
                ch.tt(n2, n2, sq1[:, :], ALU.mult)
                ch.tt(n2, n2, cols_of(nh2, s), ALU.add)
                bounded_norm(ch, nrm[:, :], n2)
                log_map(ch, sc0[:, :], s + (2 * BLOCKS + 1))
                ch.tt(sc1[:, :], sc0[:, :], g, ALU.mult)
                idle().then_inc(coef_ready, 1)
                mix(ch, sq2[:, :], y2[:, 1:2], None, s + (BLOCKS + 1), s + (BLOCKS + 1), s * 2 + (BLOCKS + 2))
                assert ch.n == PER3, ch.n

            pool.wait_ge(y2_done, 2)
            with pool.Fori(0, BLOCKS) as s:
                post2(s)
            pool.wait_ge(nh2_kept, BLOCKS)
            with pool.Fori(0, BLOCKS) as s:
                post3(s)


_INS = ['x', 'adj', 'L0_gnn_W', 'L0_gnn_b', 'L1_gnn_inlayer2', 'L1_gnn_W1', 'L1_gnn_w2', 'L1_gnn_b2', 'L1_gnn_w3',
        'L1_gnn_b3', 'L2_gnn_weight', 'L3_gnn_embed', 'L3_gnn_layer', 'L3_gnn_embed_bias', 'L3_gnn_layer_bias']


def kernel(**inputs):
    import numpy as _np
    import concourse.bacc as _bacc
    from concourse import mybir as _mybir
    from concourse.bass_utils import run_bass_kernel_spmd as _run

    nc = _bacc.Bacc("TRN2", target_bir_lowering=False, num_devices=1)
    arrays, args = {}, []
    for name in _INS:
        a = _np.ascontiguousarray(inputs[name])
        if a.ndim == 0:
            a = a.reshape(1)
        arrays[f"in_{name}_dram"] = a
        args.append(nc.dram_tensor(f"in_{name}_dram", a.shape, _mybir.dt.from_np(a.dtype), kind="ExternalInput").ap())
    out = nc.dram_tensor("out_0_dram", (4096, 128), _mybir.dt.float32, kind="ExternalOutput").ap()
    build(nc, *args, out)
    r = _run(nc, [arrays], core_ids=[0])
    return r.results[0]["out_0_dram"]
```

```python
import itertools
from contextlib import ExitStack

import concourse.bass as bass
from concourse import mybir

F32 = mybir.dt.float32
F32R = mybir.dt.float32r
BF16 = mybir.dt.bfloat16
ALU = mybir.AluOpType
ACT = mybir.ActivationFunctionType
AX = mybir.AxisListType

P = 128
N = 4096
F = 128
TILES = N // P
R4 = 4
ROWS = R4 * P
BLOCKS = N // ROWS
QUARTERS = 4
QCOLS = N // QUARTERS
QT = QCOLS // P
HALF = N // 2
LAG = 3
BUFS = 4
STEPS = BLOCKS * TILES
TAKE_SUMS, STAGE, WEIGH = 3, 4, 5
TURN_H, EMBED_H, TAKE_PQ2, LOGS2, DOT2, TANH2, MOBIUS2, LOGS2B, LATE2 = 18, 20, 22, 21, 24, 28, 33, 39, 49
TAKE_PQ3, TANH3, W3, LOGS3, TANH3B, MOBIUS3 = 6, 11, 22, 15, 33, 39
LN_EPS = 1e-5
DEG_EPS = 1e-8
H_EPS = 1e-7
MAX_TANH = 1.0 - 1e-6
MASKED = -1e9
SLOPE = 0.01
SPARES = 12
ORDER0 = [0] + list(range(BLOCKS - 1, 0, -1))
RUNS = [(b, 0, R4 * b) for b in range(1, BLOCKS)] + [(b, R4 * b, TILES) for b in ORDER0]
BELOW = BLOCKS - 1
RUN_START = [sum(j2 - j1 for _, j1, j2 in RUNS[:r]) for r in range(len(RUNS) + 1)]
UNITS0 = [(b, c) for b in ORDER0 for c in range(R4 * b // QT, QUARTERS)]
L0_USES = len(UNITS0) // QUARTERS
POST0_STEPS = 11
POST0 = []
for _o in range(BLOCKS):
    POST0.append(max(RUN_START[BELOW + _o + 1] - RUN_START[BELOW] + LAG + 4, POST0[-1] + POST0_STEPS if POST0 else 0))
GROUPS = TILES // R4
ESTEPS = TILES * GROUPS


def build(nc, x_d, adj_d, w0_d, b0_d, in2_d, w1_d, w2_d, b2_d, w3_d, b3_d, wg2_d, emb_d, lay_d, eb_d, lb_d, out_d):
    ctx = ExitStack()
    with ctx:
        def sb(name, shape, dt=F32):
            return ctx.enter_context(nc.sbuf_tensor(name, shape, dt))

        def sem(name):
            return ctx.enter_context(nc.semaphore(name))

        X = sb("X", [P, TILES, F])
        H = sb("H", [P, TILES, F])
        YA = [sb("YA_hi", [P, TILES, F], F32R), sb("YA_lo", [P, TILES, F], F32R)]
        ring = sb("ring", [P, 4, N])
        quarter = [ring[:, c, :].rearrange("p (r m) -> p r m", r=R4) for c in range(QUARTERS)]
        xw = sb("xw", [P, R4, F])
        yw = sb("yw", [P, R4, F])
        hw = sb("hw", [P, R4, F])
        early = ExitStack()
        e_over = early.enter_context(nc.sbuf_tensor("e_over", [P, N], F32))
        early.close()
        early = ExitStack()
        ones = early.enter_context(nc.sbuf_tensor("ones", [P, P], F32))
        w2B = early.enter_context(nc.sbuf_tensor("w2B", [P, P], F32))
        u2B = early.enter_context(nc.sbuf_tensor("u2B", [P, 2 * F], F32))
        W1 = early.enter_context(nc.sbuf_tensor("W1", [P, 2 * F], F32))
        u3B = early.enter_context(nc.sbuf_tensor("u3B", [P, 2, P], F32))
        early.close()
        hv = sb("hv", [P, R4, F])
        tw = sb("tw", [P, R4, F])
        hT = yw[:, :, :].rearrange("p r n -> p (r n)")
        stage_hi = sb("stage_hi", [P, R4, F], F32R)
        stage_lo = sb("stage_lo", [P, R4, F], F32R)
        oT = [sb(f"oT{e}", [P, ROWS]) for e in range(2)]
        pq = sb("pq", [P, R4, 2 * F])
        sink = sb("sink", [P, R4, F], BF16)
        sink2 = sb("sink2", [P, R4, F], BF16)
        idf = sb("idf", [P, P])
        idr = sb("idr", [P, P], F32R)
        W0 = sb("W0", [P, F])
        W2 = sb("W2", [P, F])
        EL = sb("EL", [P, 2 * F])
        IL = sb("IL", [P, 2 * F])
        w23 = sb("w23", [P, 2])
        u23 = sb("u23", [P, 2, 2])
        b0B = sb("b0B", [P, F])
        eB = sb("eB", [P, F])
        lB = sb("lB", [P, F])
        b23 = sb("b23", [P, 2])
        y2 = sb("y2", [P, 2])
        nhalf = sb("nhalf", [P, TILES])
        half = sb("half", [P, R4])
        one = sb("one", [P, R4])
        mone = sb("mone", [P, R4])
        deg = sb("deg", [P, TILES])
        deg2 = sb("deg2", [P, TILES])
        d0 = sb("d0", [P, TILES])
        d2 = sb("d2", [P, TILES])
        f1 = sb("f1", [P, TILES])
        nh2 = sb("nh2", [P, TILES])
        dpart = sb("dpart", [P, QUARTERS, R4])
        st = sb("st", [P, R4, 6])
        mv = sb("mv", [P, R4, 2])
        ve = sb("ve", [P, R4])
        rs = sb("rs", [P, R4])
        mx = sb("mx", [P, 2])
        negm = sb("negm", [P, R4])
        mf1 = sb("mf1", [P, TILES])
        rsum = sb("rsum", [P, 2, 2, R4])
        rcp = sb("rcp", [P, R4])
        sq1 = sb("sq1", [P, R4])
        sq2 = sb("sq2", [P, R4])
        sq3 = sb("sq3", [P, R4])
        dot = sb("dot", [P, R4])
        ln1 = sb("ln1", [P, R4])
        ln2 = sb("ln2", [P, R4])
        th = sb("th", [P, R4])
        nrm = sb("nrm", [P, R4])
        nrc = sb("nrc", [P, R4])
        nth = sb("nth", [P, R4])
        sc0 = sb("sc0", [P, R4])
        sc1 = sb("sc1", [P, R4])
        al = sb("al", [P, R4])
        be = sb("be", [P, R4])
        ps = sb("ps", [P, 8, R4])
        spare = sb("spare", [P, 3, SPARES])

        early = ExitStack()
        in2T = early.enter_context(nc.sbuf_tensor("in2T", [P, 2, 2, ROWS], F32))
        products1 = early.enter_context(nc.sbuf_tensor("products1", [P, TILES // 2, 2 * F], BF16))
        early.close()
        early = ExitStack()
        ET = early.enter_context(nc.sbuf_tensor("ET", [P, BUFS, R4, P], F32))
        R = early.enter_context(nc.sbuf_tensor("R", [P, HALF], F32))
        early.close()
        hi = sb("hi", [P, BUFS, ROWS], F32R)
        lo = sb("lo", [P, BUFS, ROWS], F32R)
        early = ExitStack()
        f2B = early.enter_context(nc.sbuf_tensor("f2B", [P, N], F32))
        e_beside = early.enter_context(nc.sbuf_tensor("e_beside", [P, N], F32))
        early.close()
        unwanted = e_beside[:, :].bitcast(BF16)
        LG = [e_beside[:, :], ring[:, 2, :], ring[:, 3, :], e_over[:, :]]
        YB = [sb("YB_hi", [P, TILES, F], F32R), sb("YB_lo", [P, TILES, F], F32R)]
        FEATURES = [YA, YA, YB]

        in2 = [H[:, :, :].rearrange("p (t k) f -> p t (k f)", k=2),
               e_beside[:, :].rearrange("p (t m) -> p t m", m=2 * F)]

        TP = [ctx.enter_context(nc.psum_tensor(f"TP{i}", [P, ROWS], F32)) for i in range(BUFS)]
        OT = [ctx.enter_context(nc.psum_tensor(f"OT{i}", [P, ROWS], F32)) for i in range(2)]
        PP = ctx.enter_context(nc.psum_tensor("PP", [P, 2, ROWS], F32))
        PQ = PP[:, :, :].rearrange("p a (r n) -> p (a r) n", n=2 * F)

        sums_in = sem("sums_in")
        consts_in = sem("consts_in")
        x_in = sem("x_in")
        in2_in = [sem(f"in2_in{i}") for i in range(4)]
        adj_in = [sem(f"adj_in{i}") for i in range(4)]
        consts = sem("consts")
        ident = sem("ident")
        ident_r = sem("ident_r")
        w2_spread = sem("w2_spread")
        u_done = sem("u_done")
        u2_copied = sem("u2_copied")
        f1_summed = sem("f1_summed")
        f1_ready = sem("f1_ready")
        u_copied = sem("u_copied")
        u_spread = sem("u_spread")
        y2_done = sem("y2_done")
        in2_turned = sem("in2_turned")
        in2_copied = sem("in2_copied")
        f_done = sem("f_done")
        f_copied = sem("f_copied")
        summed = sem("summed")
        summed_act = sem("summed_act")
        part_kept = sem("part_kept")
        deg_ready = sem("deg_ready")
        d_step = sem("d_step")
        d_ready = sem("d_ready")
        x_new = sem("x_new")
        x_kept = sem("x_kept")
        bn_stat = sem("bn_stat")
        bn_agg = sem("bn_agg")
        var_ready = sem("var_ready")
        pow_done = sem("pow_done")
        rstd_ready = sem("rstd_ready")
        normed = sem("normed")
        h_ready = sem("h_ready")
        yhi_ready = sem("yhi_ready")
        y_ready = sem("y_ready")
        turned = sem("turned")
        hi_done = sem("hi_done")
        lo_done = sem("lo_done")
        spent = sem("spent")
        staged = sem("staged")
        oT_ready = sem("oT_ready")
        post_done = sem("post_done")
        scaled = sem("scaled")
        biased0 = sem("biased0")
        mf1_ready = sem("mf1_ready")
        bent = sem("bent")
        bent_added = sem("bent_added")
        biased = sem("biased")
        masked = sem("masked")
        m_ready = sem("m_ready")
        exp_done = sem("exp_done")
        et_turned = sem("et_turned")
        et_copied = sem("et_copied")
        et_used = sem("et_used")
        l1_taken = sem("l1_taken")
        rsum_added = sem("rsum_added")
        rcp_ready = sem("rcp_ready")
        hw_ready = sem("hw_ready")
        hT_turned = sem("hT_turned")
        hT_ready = sem("hT_ready")
        pq_done = sem("pq_done")
        pq_ready = sem("pq_ready")
        pq_used = sem("pq_used")
        q_kept = sem("q_kept")
        sq1_ready = sem("sq1_ready")
        sq2_ready = sem("sq2_ready")
        sq3_ready = sem("sq3_ready")
        dot_ready = sem("dot_ready")
        nrm_ready = sem("nrm_ready")
        ln_ready = sem("ln_ready")
        nth_ready = sem("nth_ready")
        th_ready = sem("th_ready")
        coef_ready = sem("coef_ready")
        mix_ready = sem("mix_ready")
        mixed = sem("mixed")
        w_ready = sem("w_ready")
        s_ready = sem("s_ready")
        pool_step = sem("pool_step")
        bias_scaled = sem("bias_scaled")
        w_scaled = sem("w_scaled")
        y3_scaled = sem("y3_scaled")
        nh2_kept = sem("nh2_kept")
        il_ready = sem("il_ready")
        x_final = sem("x_final")
        stored = sem("stored")

        block = ctx.enter_context(nc.Block())

        ROWTILE_USES = BLOCKS + L0_USES
        QUARTER_USES = [None,
                        [ROWTILE_USES + TILES // 2] * 2 + [ROWTILE_USES] * 2,
                        [ROWTILE_USES + BLOCKS + TILES // 2] * 2 + [ROWTILE_USES + BLOCKS] * 2]
        SUMS_DMAS, CONST_DMAS = 5, 8
        PER2 = 63
        PER3 = 47

        def tiles_of(t, s):
            return t[:, bass.ds(s * R4, R4), :]

        def cols_of(t, s):
            return t[:, bass.ds(s * R4, R4)]

        def per_row(t):
            return t.rearrange("p (r o) -> p r o", o=1).to_broadcast([P, R4, F])

        def per_col(t):
            return t.rearrange("p (o n) -> p o n", o=1).to_broadcast([P, R4, F])

        def spare_column(e):
            return (spare[:, e, i:i + 1] for i in itertools.cycle(range(SPARES)))

        def column(d):
            return d.rearrange("(n a) -> n a", a=1)

        def row(d):
            return d.rearrange("(a n) -> a n", a=1)

        def part_of(b):
            return H[:, b * R4:(b + 1) * R4, :].rearrange("p r n -> p (r n)")

        def on_act(s, c):
            return s > 0 and c % 2 == 1

        ACT_QUARTERS = [(s, c) for s in range(BLOCKS) for c in range(QUARTERS) if on_act(s, c)]
        DVE_QUARTERS = [(s, c) for s in range(BLOCKS) for c in range(QUARTERS) if not on_act(s, c)]

        def run_of_block(s):
            return s - 1

        def column_blocks_below(s, c):
            return min(max(R4 * s - QT * c, 0), QT)

        def settle(carrier, s, value):
            eng, carry = carrier
            eng.wait_ge(s, value)
            if not isinstance(value, int):
                carry()

        def blocks_loop(eng, body):
            body(0, True)
            with eng.Fori(1, BLOCKS // 2) as q:
                body(q, False)

        @block.sync
        def _(sp):
            def load(s, c):
                sp.dma_start(quarter[c], adj_d[bass.ds(s * ROWS, ROWS), c * QCOLS:(c + 1) * QCOLS]
                             .rearrange("(r p) m -> p r m", p=P)).then_inc(adj_in[c], 16)

            def load_pass(base, after):
                for c in range(QUARTERS):
                    after(c)
                    load(0, c)
                with sp.Fori(1, BLOCKS) as s:
                    for c in range(QUARTERS):
                        sp.wait_ge(turned, s * TILES + (base - TILES + QT * (c + 1)))
                        load(s, c)

            def quarter_used(s, c):
                if on_act(s, c):
                    sp.wait_ge(summed_act, ACT_QUARTERS.index((s, c)) + 1)
                else:
                    sp.wait_ge(summed, DVE_QUARTERS.index((s, c)) + 1)
                if column_blocks_below(s, c):
                    sp.wait_ge(turned, RUN_START[run_of_block(s)] + QT * c + column_blocks_below(s, c))

            for i in range(4):
                sp.dma_start(in2[i // 2][:, (i % 2) * 2 * R4:(i % 2 + 1) * 2 * R4, :],
                             in2_d[i * 2 * ROWS:(i + 1) * 2 * ROWS, :].rearrange("(t p) m -> p t m", p=P))\
                    .then_inc(in2_in[i], 16)
            for c in range(QUARTERS):
                load(0, c)
                if c == 1:
                    sp.dma_start(X[:, :, :], x_d.rearrange("(t p) f -> p t f", p=P)).then_inc(x_in, 16)
            for dst, src in ((W0, w0_d), (W2, wg2_d), (EL[:, 0:F], emb_d), (EL[:, F:2 * F], lay_d[0:F, :]),
                             (IL[:, F:2 * F], lay_d[F:2 * F, :]), (b0B, row(b0_d).to_broadcast([P, F])),
                             (eB, row(eb_d).to_broadcast([P, F])), (lB, row(lb_d).to_broadcast([P, F]))):
                sp.dma_start(dst[:, :], src).then_inc(consts_in, 16)
            for s in range(1, BLOCKS):
                for c in range(QUARTERS):
                    quarter_used(s - 1, c)
                    load(s, c)
            unit_end = [RUN_START[BELOW + ORDER0.index(b)] + QT * (c + 1) - R4 * b for b, c in UNITS0]
            for n, (b, c) in enumerate(UNITS0):
                slot = n % QUARTERS
                if n < QUARTERS:
                    quarter_used(BLOCKS - 1, slot)
                else:
                    sp.wait_ge(turned, unit_end[n - QUARTERS])
                first = max(b * ROWS - c * QCOLS, 0)
                sp.dma_start(quarter[slot][:, :, first:QCOLS],
                             adj_d[b * ROWS:(b + 1) * ROWS, c * QCOLS + first:(c + 1) * QCOLS]
                             .rearrange("(r p) m -> p r m", p=P)).then_inc(adj_in[slot], 16)
            for e in range(2):
                sp.wait_ge(turned, unit_end[len(UNITS0) - QUARTERS + e])
                sp.dma_start(ring[:, e, :], adj_d[e * P:(e + 1) * P, :]).then_inc(adj_in[e], 16)
            with sp.Fori(1, TILES // 2) as u:
                for e in range(2):
                    sp.wait_ge(biased, u * 4 + (2 * e - 2))
                    sp.dma_start(ring[:, e, :], adj_d[bass.ds(u * (2 * P) + e * P, P), :]).then_inc(adj_in[e], 16)

            def after_layer1(c):
                if c < 2:
                    sp.wait_ge(biased, 2 * (TILES - 2 + c + 1))
                else:
                    sp.wait_ge(et_turned, ESTEPS - GROUPS * (4 - c))
            load_pass(STEPS, after_layer1)
            load_pass(2 * STEPS, lambda c: sp.wait_ge(turned, 2 * STEPS - TILES + QT * (c + 1)))
            out_v = out_d.rearrange("(t p) f -> p t f", p=P)
            for s in range(BLOCKS):
                sp.wait_ge(x_final, s + 1)
                sp.dma_start(out_v[:, s * R4:(s + 1) * R4, :], X[:, s * R4:(s + 1) * R4, :]).then_inc(stored, 16)
            sp.wait_ge(stored, 16 * BLOCKS)

        @block.tensor
        def _(pe):
            pe.wait_ge(ident, 2)
            pe.wait_ge(il_ready, 1)
            pe.wait_ge(sums_in, 16 * SUMS_DMAS)
            for k in range(2):
                pe.matmul(PP[:, 1, 2 * k:2 * k + 2], W1[:, k * F:(k + 1) * F], w23[:, :], start=True, stop=True)
            pe.wait_ge(w2_spread, 1)
            pe.matmul(PP[:, 0, 0:2 * F], w2B[:, :], W1[:, :], start=True, stop=True).then_inc(u_done, 1)
            pe.wait_ge(u_spread, 1)

            for s in range(BLOCKS):
                e = s % 2
                if e == 0:
                    pe.wait_ge(in2_in[s // 2], 16)
                for k in range(2):
                    if s > 1:
                        pe.wait_ge(in2_copied, s * 2 + (k - 3))
                    for r in range(R4):
                        mm = pe.transpose(TP[2 * e + k][:, r * P:(r + 1) * P],
                                          in2[s // 4][:, s % 4 * R4 + r, k * F:(k + 1) * F], idf[:, :])
                    mm.then_inc(in2_turned, 1)
                pe.wait_ge(in2_copied, s * 2 + 2)
                if s > 1:
                    pe.wait_ge(f_copied, s - 1)
                for k in range(2):
                    mm = pe.matmul(OT[e][:, :], u3B[:, k, :], in2T[:, e, k, :], start=(k == 0), stop=(k == 1))
                mm.then_inc(f_done, 1)

            def turn(p, s, j):
                c = j // QT
                if j % QT == 0:
                    pe.wait_ge(adj_in[c], s * 16 + 16 * (QUARTER_USES[p][c] + 1))
                for r in range(R4):
                    mm = pe.transpose(TP[j % BUFS][:, r * P:(r + 1) * P],
                                      quarter[c][:, r, (j % QT) * P:(j % QT + 1) * P], idf[:, :])
                mm.then_inc(turned, 1)

            def product(p, s, e, j, first_block):
                y_hi, y_lo = FEATURES[p]
                if first_block and j % R4 == 0:
                    pe.wait_ge(y_ready, p * BLOCKS + j // R4 + 1)
                if j == 0:
                    if p == 1 and first_block:
                        pe.wait_ge(l1_taken, BLOCKS - 1 + e)
                    else:
                        pe.wait_ge(oT_ready, s + (p * BLOCKS - 1))
                pe.wait_ge(lo_done, s * TILES + (p * STEPS + j + 1))
                if p == 1 and j == TILES - 1:
                    pe.wait_ge(staged, s + 1)
                    for r in range(R4):
                        for part in (stage_hi, stage_lo):
                            pe.matmul(OT[e][:, r * P:(r + 1) * P], part[:, r, :], idr[:, :], start=False, stop=False,
                                      skip_group_check=True)
                a_hi, a_lo = hi[:, j % BUFS, :], lo[:, j % BUFS, :]
                pe.matmul(OT[e][:, :], y_hi[:, j, :], a_hi, start=(j == 0), stop=False)
                pe.matmul(OT[e][:, :], y_hi[:, j, :], a_lo, start=False, stop=False)
                pe.matmul(OT[e][:, :], y_lo[:, j, :], a_hi, start=False, stop=(j == TILES - 1)).then_inc(spent, 1)

            def weigh(p, s, e):
                pe.wait_ge(oT_ready, s + (p * BLOCKS + 1))
                if p == 0:
                    if isinstance(s, int) and s == 0:
                        pe.wait_ge(f_copied, BLOCKS)
                    else:
                        pe.wait_ge(scaled, s)
                else:
                    if not (p == 1 and isinstance(s, int) and s == 0):
                        pe.wait_ge(pq_ready, s + (p - 1) * BLOCKS)
                for r in range(R4):
                    if p < 2:
                        mm = pe.matmul(PP[:, 0, r * P:(r + 1) * P], oT[e][:, r * P:(r + 1) * P],
                                       (W0, W2)[p][:, :], start=True, stop=True)
                    else:
                        mm = pe.matmul(PQ[:, r, :], oT[e][:, r * P:(r + 1) * P], IL[:, :], start=True, stop=True)
                mm.then_inc(post_done, 1)

            def turn_h(s):
                pe.wait_ge(hw_ready, s + 1)
                for r in range(R4):
                    mm = pe.transpose(PP[:, 1, r * P:(r + 1) * P], hw[:, r, :], idf[:, :])
                mm.then_inc(hT_turned, 1)

            def embed_h(s):
                pe.wait_ge(hT_ready, s + 1)
                for r in range(R4):
                    mm = pe.matmul(PQ[:, r, :], hT[:, r * P:(r + 1) * P], EL[:, :], start=True, stop=True)
                mm.then_inc(pq_done, 1)

            def stages(p, block_of, j):
                s, e = block_of
                if j == WEIGH:
                    weigh(p, s, e)
                if p == 1 and j == TURN_H:
                    turn_h(s)
                if p == 1 and j == EMBED_H:
                    embed_h(s)

            def gcn_pass(p):
                def body(q, first):
                    for k in range(2 * TILES):
                        e, j = divmod(k, TILES)
                        turn(p, q * 2 + e, j)
                        if k >= LAG:
                            e2, j2 = divmod(k - LAG, TILES)
                            product(p, q * 2 + e2, e2, j2, first and e2 == 0)
                        elif not first:
                            product(p, q * 2 - 1, 1, TILES + k - LAG, False)
                        elif p == 2:
                            product(1, BLOCKS - 1, 1, TILES + k - LAG, False)
                        if first and e == 0:
                            if p == 2:
                                stages(1, (BLOCKS - 1, 1), j)
                        else:
                            stages(p, (q * 2 + (e - 1), 1 - e), j)

                blocks_loop(pe, body)
                if p == 2:
                    for j in range(TILES - LAG, TILES):
                        product(p, BLOCKS - 1, 1, j, False)
                    weigh(p, BLOCKS - 1, 1)

            def turn0(k, r, j):
                b, j1, _ = RUNS[r]
                c = j // QT
                if r < BELOW:
                    slot, uses = c, b
                else:
                    slot, uses = UNITS0.index((b, c)) % QUARTERS, BLOCKS + UNITS0.index((b, c)) // QUARTERS
                if j % QT == 0 or j == j1:
                    pe.wait_ge(adj_in[slot], 16 * (uses + 1))
                for i in range(R4):
                    mm = pe.transpose(TP[k % BUFS][:, i * P:(i + 1) * P],
                                      quarter[slot][:, i, (j % QT) * P:(j % QT + 1) * P], idf[:, :])
                mm.then_inc(turned, 1)

            def product0(k, r, j):
                b, j1, j2 = RUNS[r]
                if j == j1:
                    if r < 2:
                        pe.wait_ge(f_copied, BLOCKS)
                    elif r < BELOW + 2:
                        pe.wait_ge(part_kept, r - 1)
                    else:
                        pe.wait_ge(oT_ready, r - BELOW - 1)
                if j % R4 == 0 and r <= BELOW:
                    pe.wait_ge(y_ready, j // R4 + 1)
                pe.wait_ge(lo_done, k + 1)
                y_hi, y_lo = YA
                if r >= BELOW and j == j2 - 1:
                    for i in range(R4):
                        for y in YA:
                            pe.matmul(OT[r % 2][:, i * P:(i + 1) * P], y[:, b * R4 + i, :], idr[:, :], start=False,
                                      stop=False, skip_group_check=True)
                a_hi, a_lo = hi[:, k % BUFS, :], lo[:, k % BUFS, :]
                pe.matmul(OT[r % 2][:, :], y_hi[:, j, :], a_hi, start=(j == j1), stop=False)
                pe.matmul(OT[r % 2][:, :], y_hi[:, j, :], a_lo, start=False, stop=False)
                pe.matmul(OT[r % 2][:, :], y_lo[:, j, :], a_hi, start=False, stop=(j == j2 - 1)).then_inc(spent, 1)

            pe.wait_ge(ident_r, 1)
            pe.wait_ge(consts_in, 16 * CONST_DMAS)
            steps = [(r, j) for r, (_, j1, j2) in enumerate(RUNS) for j in range(j1, j2)]
            for k, (r, j) in enumerate(steps):
                turn0(k, r, j)
                if k >= LAG:
                    product0(k - LAG, *steps[k - LAG])
                if k - RUN_START[BELOW] + 2 in POST0:
                    o = POST0.index(k - RUN_START[BELOW] + 2)
                    weigh(0, o, o % 2)
            for k in range(STEPS - LAG, STEPS):
                product0(k, *steps[k])
            weigh(0, BLOCKS - 1, (BLOCKS - 1) % 2)

            def turn_e(t, i, g):
                if g % (GROUPS // 2) == 0:
                    pe.wait_ge(exp_done, t * 2 + (g // (GROUPS // 2) + 1))
                for k in range(R4):
                    mm = pe.transpose(TP[g % BUFS][:, k * P:(k + 1) * P],
                                      LG[i % 4][:, (g * R4 + k) * P:(g * R4 + k + 1) * P], idf[:, :])
                mm.then_inc(et_turned, 1)

            def product_e(t, s, i, g, first_tile, first):
                if first_tile and g == 0:
                    pe.wait_ge(h_ready, BLOCKS)
                if i % R4 == 0 and g == 0:
                    if first:
                        pe.wait_ge(oT_ready, BLOCKS)
                    else:
                        pe.wait_ge(l1_taken, s - 1)
                pe.wait_ge(et_copied, t * GROUPS + (g + 1))
                r = i % R4
                for k in range(R4):
                    mm = pe.matmul(OT[i // R4][:, r * P:(r + 1) * P], ET[:, g % BUFS, k, :], H[:, g * R4 + k, :],
                                   start=(g == 0 and k == 0), stop=(g == GROUPS - 1 and k == R4 - 1))
                mm.then_inc(et_used, 1)

            def attend(q, first):
                for i in range(2 * R4):
                    for g in range(GROUPS):
                        turn_e(q * 8 + i, i, g)
                        i2, g2 = (i, g - 2) if g >= 2 else (i - 1, g + GROUPS - 2)
                        if i2 >= 0:
                            product_e(q * 8 + i2, q * 2 + i2 // R4, i2, g2, first and i2 == 0, first)
                        elif not first:
                            product_e(q * 8 - 1, q * 2 - 1, 7, g2, False, False)

            blocks_loop(pe, attend)
            for g in range(GROUPS - 2, GROUPS):
                product_e(TILES - 1, BLOCKS - 1, 7, g, False, False)

            gcn_pass(1)
            gcn_pass(2)

        @block.scalar
        def _(act):
            act_spare = spare_column(0)
            act_carry = (act, lambda: act.activation(next(act_spare), nhalf[:, 0:1], ACT.Copy))
            for dst, src in ((W1, w1_d), (w23[:, 0:1], column(w2_d)), (w23[:, 1:2], column(w3_d)),
                             (b23[:, 0:1], row(b2_d).to_broadcast([P, 1])),
                             (b23[:, 1:2], row(b3_d).to_broadcast([P, 1]))):
                act.dma_start(dst[:, :], src).then_inc(sums_in, 16)
            act.wait_ge(ident, 2)
            act.activation(idr[:, :], idf[:, :], ACT.Copy).then_inc(ident_r, 1)
            act.wait_ge(consts, 5)
            act.wait_ge(sums_in, 16 * SUMS_DMAS)
            act.activation(w2B[:, :], ones[:, :], ACT.Copy, scale=w23[:, 0:1]).then_inc(w2_spread, 1)
            act.wait_ge(u_done, 1)
            act.activation(u2B[:, :], PP[:, 0, 0:2 * F], ACT.Copy).then_inc(u2_copied, 1)
            act.activation(u23[:, :, :].rearrange("p a b -> p (a b)"), PP[:, 1, 0:4], ACT.Copy).then_inc(u_copied, 1)
            act.wait_ge(u_copied, 1)
            act.wait_ge(consts, 5)
            act.activation(u3B[:, 0, :], ones[:, :], ACT.Copy, scale=u23[:, 0, 1:2])
            act.activation(u3B[:, 1, :], ones[:, :], ACT.Copy, scale=u23[:, 1, 1:2]).then_inc(u_spread, 1)
            for s in range(BLOCKS):
                e = s % 2
                for k in range(2):
                    act.wait_ge(in2_turned, s * 2 + (k + 1))
                    act.activation(in2T[:, e, k, :], TP[2 * e + k][:, :], ACT.Copy).then_inc(in2_copied, 1)
                act.wait_ge(f_done, s + 1)
                act.activation(f2B[:, s * ROWS:(s + 1) * ROWS], OT[e][:, :], ACT.Identity, bias=b23[:, 1:2])\
                   .then_inc(f_copied, 1)

            act.wait_ge(consts_in, 16 * CONST_DMAS)
            act.activation(sink[:, 0, :], eB[:, :], ACT.Square, accum_out=y2[:, 0:1]).then_inc(y2_done, 1)
            act.wait_ge(y2_done, 1)
            act.activation(sink[:, 1, :], lB[:, :], ACT.Square, accum_out=y2[:, 1:2]).then_inc(y2_done, 1)

            def row_sum(s, c, r):
                n = ACT_QUARTERS.index((s, c))
                if n > 1 and r == 0:
                    act.wait_ge(summed_act, n - 1)
                if c == 1 and r == 0:
                    act.wait_ge(deg_ready, s)
                if r == 0:
                    act.wait_ge(adj_in[c], 16 * (s + 1))
                region = n % 2 * R4 + r
                ins = act.activation(unwanted[:, region * QCOLS:(region + 1) * QCOLS], quarter[c][:, r, :], ACT.Copy,
                                     accum_out=dpart[:, c, r:r + 1])
                if r == R4 - 1:
                    ins.then_inc(summed_act, 1)

            def split_hi0(k):
                act.wait_ge(turned, k + 1)
                if k < BUFS:
                    act.wait_ge(f_done, BLOCKS)
                else:
                    act.wait_ge(spent, k - BUFS + 1)
                act.activation(hi[:, k % BUFS, :], TP[k % BUFS][:, :], ACT.Copy).then_inc(hi_done, 1)

            def keep_part(r):
                act.wait_ge(spent, RUN_START[r + 1])
                act.activation(part_of(RUNS[r][0]), OT[r % 2][:, :], ACT.Copy).then_inc(part_kept, 1)

            def bend(t, i, c):
                half_of = slice(c * HALF, (c + 1) * HALF)
                act.activation(LG[i % 4][:, half_of], f2B[:, half_of], ACT.Relu, bias=mf1[:, bass.ds(t, 1)],
                               scale=SLOPE - 1.0).then_inc(bent, 1)

            act.wait_ge(mf1_ready, 1)
            for s in range(1, BLOCKS):
                r = run_of_block(s)
                for c in range(QUARTERS):
                    for i in range(QT):
                        if i < column_blocks_below(s, c):
                            split_hi0(RUN_START[r] + c * QT + i)
                        if r and c * QT + i == LAG:
                            keep_part(r - 1)
                        if on_act(s, c) and i % 2:
                            row_sum(s, c, i // 2)
            act.wait_ge(summed_act, len(ACT_QUARTERS))
            for c in range(2):
                bend(0, 0, c)
            for k in range(RUN_START[BELOW], STEPS):
                split_hi0(k)
                if k == RUN_START[BELOW] + LAG:
                    keep_part(BELOW - 1)

            def split_hi(p, s, j, first):
                act.wait_ge(turned, s * TILES + (p * STEPS + j + 1))
                if first and j < BUFS and p == 1:
                    act.wait_ge(et_used, ESTEPS)
                else:
                    act.wait_ge(spent, s * TILES + (p * STEPS + j - BUFS + 1))
                act.activation(hi[:, j % BUFS, :], TP[j % BUFS][:, :], ACT.Copy).then_inc(hi_done, 1)

            def take_sums(p, s, e):
                act.wait_ge(spent, s * TILES + (p * STEPS + TILES))
                act.activation(oT[e][:, :], OT[e][:, :], ACT.Copy).then_inc(oT_ready, 1)

            def squares(src, dst, ready, part=None):
                for r in range(R4) if part is None else (2 * part, 2 * part + 1):
                    ins = act.activation(sink[:, r, :], src[:, r, 0:F], ACT.Square, accum_out=dst[:, r:r + 1])
                if part != 0:
                    ins.then_inc(ready, 1)

            def take_hT(s):
                act.wait_ge(hT_turned, s + 1)
                act.activation(hT, PP[:, 1, :], ACT.Copy).then_inc(hT_ready, 1)

            def take_pq(p, s):
                if p == 1:
                    act.wait_ge(pq_done, s + 1)
                else:
                    act.wait_ge(post_done, s + (2 * BLOCKS + 1))
                if not (p == 1 and isinstance(s, int) and s == 0):
                    act.wait_ge(pq_used, s + (p - 1) * BLOCKS)
                    if p == 1:
                        act.wait_ge(q_kept, s)
                    else:
                        act.wait_ge(q_kept, BLOCKS)
                act.activation(pq[:, :, :], PQ[:, :, :], ACT.Copy).then_inc(pq_ready, 1)

            def logs(n):
                act.wait_ge(nrm_ready, n)
                act.activation(ln1[:, :], nrc[:, :], ACT.Ln, bias=1.0)
                act.activation(ln2[:, :], nrc[:, :], ACT.Ln, bias=1.0, scale=-1.0).then_inc(ln_ready, 1)

            def tanh(n):
                act.wait_ge(nth_ready, n)
                act.activation(th[:, :], nth[:, :], ACT.Tanh).then_inc(th_ready, 1)

            L2_LOGS, L2_TANHS = 2 * BLOCKS, BLOCKS

            def post2(s, j):
                if j == TURN_H - 1:
                    act.wait_ge(hw_ready, s + 1)
                    squares(hw, sq1, sq1_ready, 0)
                if j == TURN_H:
                    squares(hw, sq1, sq1_ready, 1)
                if j == TURN_H + 1:
                    take_hT(s)
                if j == TAKE_PQ2:
                    take_pq(1, s)
                if j == TAKE_PQ2 + 1:
                    act.wait_ge(pq_ready, s + 1)
                    squares(pq, sq2, sq2_ready, 0)
                if j == TAKE_PQ2 + 2:
                    squares(pq, sq2, sq2_ready, 1)
                if j == LOGS2:
                    logs(s * 2 + 1)
                if j == TANH2:
                    tanh(s + 1)
                if j == MOBIUS2 + 3:
                    act.wait_ge(mixed, s + 1)
                    squares(hv, sq3, sq3_ready, 0)
                if j == MOBIUS2 + 4:
                    squares(hv, sq3, sq3_ready, 1)
                if j == LOGS2B:
                    logs(s * 2 + 2)

            def post3(s, j):
                if j == TAKE_PQ3:
                    take_pq(2, s)
                if j == TAKE_PQ3 + 1:
                    act.wait_ge(pq_ready, s + (BLOCKS + 1))
                    squares(pq, sq1, sq1_ready, 0)
                if j == TAKE_PQ3 + 2:
                    squares(pq, sq1, sq1_ready, 1)
                if j == TANH3:
                    tanh(s * 2 + (L2_TANHS + 1))
                if j == LOGS3:
                    logs(s + (L2_LOGS + 1))
                if j == W3 + 3:
                    act.wait_ge(w_ready, s + 1)
                    squares(hv, sq2, sq2_ready, 0)
                if j == W3 + 4:
                    squares(hv, sq2, sq2_ready, 1)
                if j == TANH3B:
                    tanh(s * 2 + (L2_TANHS + 2))

            def gcn_pass(p):
                def stages(p, s, e, j):
                    if j == TAKE_SUMS:
                        take_sums(p, s, e)
                    (None, post2, post3)[p](s, j)

                def body(q, first):
                    for k in range(2 * TILES):
                        e, j = divmod(k, TILES)
                        split_hi(p, q * 2 + e, j, first and e == 0)
                        if not first:
                            stages(p, q * 2 + (e - 2), e, TILES + j)
                        if not (first and e == 0):
                            stages(p, q * 2 + (e - 1), 1 - e, j)
                        elif p == 2:
                            stages(1, BLOCKS - 2, 0, TILES + j)
                            stages(1, BLOCKS - 1, 1, j)
                        if p == 2 and first and k == TILES - 1:
                            for late in range(TILES, 2 * TILES):
                                stages(1, BLOCKS - 1, 1, late)

                blocks_loop(act, body)
                if p == 2:
                    for j in range(2 * TILES):
                        if j < TILES:
                            stages(p, BLOCKS - 2, 0, TILES + j)
                        stages(p, BLOCKS - 1, 1, j)

            def exps(t, i, c):
                lg = LG[i % 4][:, c * HALF:(c + 1) * HALF]
                act.wait_ge(m_ready, t + 1)
                act.activation(lg, lg, ACT.Exp, bias=negm[:, i % 4:i % 4 + 1],
                               accum_out=rsum[:, i // R4, c, i % R4:i % R4 + 1]).then_inc(exp_done, 1)

            def take_e(t, g, first_tile):
                act.wait_ge(et_turned, t * GROUPS + (g + 1))
                if first_tile and g < BUFS:
                    act.wait_ge(spent, STEPS)
                else:
                    act.wait_ge(et_used, t * GROUPS + (g - BUFS + 1))
                act.activation(ET[:, g % BUFS, :, :].rearrange("p k m -> p (k m)"), TP[g % BUFS][:, :], ACT.Copy)\
                   .then_inc(et_copied, 1)

            def beside(t, i, first_tile, parts):
                for g in range(GROUPS):
                    if g % 2:
                        parts[g // 2]()
                    take_e(t, g, first_tile)

            def attend(q, first):
                for i in range(2 * R4):
                    t = q * 8 + i

                    def bend_part(c):
                        if not first:
                            settle(act_carry, et_turned, t * GROUPS + ((c + 1) * (GROUPS // 2) - 4 * GROUPS))
                        elif i == 3:
                            act.wait_ge(post_done, BLOCKS)
                        elif i > 3:
                            act.wait_ge(et_turned, (i - 4) * GROUPS + (c + 1) * (GROUPS // 2))
                        elif i:
                            act.wait_ge(turned, STEPS)
                        bend(t, i, c)

                    if first and i < 3:
                        for c in range(2):
                            if i:
                                bend_part(c)
                    elif first and i == 3:
                        for c in range(2):
                            exps(0, 0, c)
                            bend_part(c)
                    else:
                        j = (i - 3) % 8
                        beside(t - 4, (i - 4) % 8, first and i == 4,
                               (lambda: exps(t - 3, j, 0), lambda: exps(t - 3, j, 1),
                                lambda: bend_part(0), lambda: bend_part(1)))

            blocks_loop(act, attend)
            for t in range(TILES - 3, TILES):
                beside(t - 1, (t - 1) % 8, False,
                       (lambda: exps(t, t % 8, 0), lambda: exps(t, t % 8, 1), lambda: None, lambda: None))
            for g in range(GROUPS):
                take_e(TILES - 1, g, False)

            gcn_pass(1)
            gcn_pass(2)

        @block.vector
        def _(dve):
            dve_spare = spare_column(1)
            dve_carry = (dve, lambda: dve.memset(next(dve_spare), 0.0))

            def ln_sums(prep, s, part):
                if part == 0:
                    dve.wait_ge(x_new, s + (prep * BLOCKS + 1))
                for r in (2 * part, 2 * part + 1):
                    ins = dve.bn_stats(st[:, r, :], xw[:, r, :])
                if part:
                    ins.then_inc(bn_stat, 1)

            def ln_variance(prep, s):
                n = s + (prep * BLOCKS + 1)
                settle(dve_carry, bn_stat, n)
                for r in range(R4):
                    ins = dve.bn_aggr(mv[:, r, :], st[:, r, :])
                ins.then_inc(bn_agg, 1)
                dve.wait_ge(bn_agg, n)
                dve.tensor_scalar(ve[:, :], mv[:, :, 1], LN_EPS, None, ALU.add).then_inc(var_ready, 1)

            def ln_scale(prep, s, part):
                if part == 0:
                    dve.wait_ge(rstd_ready, s + (prep * BLOCKS + 1))
                for r in (2 * part, 2 * part + 1):
                    ins = dve.tensor_scalar(yw[:, r, :], xw[:, r, :], mv[:, r, 0:1], rs[:, r:r + 1],
                                            ALU.subtract, ALU.mult)
                if part:
                    ins.then_inc(normed, 1)

            def ln_relu(prep, s, b):
                dve.wait_ge(normed, s + (prep * BLOCKS + 1))
                if prep == 1:
                    dve.tensor_scalar(tiles_of(H, b), yw[:, :, :], 0.0, None, ALU.max).then_inc(h_ready, 1)
                elif prep == 3:
                    dve.tensor_scalar(hw[:, :, :], yw[:, :, :], 0.0, None, ALU.max).then_inc(hw_ready, 1)
                else:
                    dve.tensor_scalar(tiles_of(YA[0], s), yw[:, :, :], 0.0, None, ALU.max).then_inc(yhi_ready, 1)

            def ln_lo(prep, s):
                dve.wait_ge(yhi_ready, s + (prep // 2 * BLOCKS + 1))
                dve.scalar_tensor_tensor(out=tiles_of(YA[1], s), in0=yw[:, :, :], scalar=0.0,
                                         in1=tiles_of(YA[0], s).bitcast(F32), op0=ALU.max, op1=ALU.subtract)\
                   .then_inc(y_ready, 1)

            def keep_x(prep, s):
                dve.tensor_scalar(tiles_of(X, s), xw[:, :, :], 1.0, None, ALU.mult).then_inc(x_kept, 1)

            def stage(p, s):
                dve.wait_ge(spent, s * TILES + p * STEPS)
                dve.tensor_scalar(stage_hi[:, :, :], tiles_of(YA[0], s).bitcast(F32), 1.0, None, ALU.mult)
                dve.tensor_scalar(stage_lo[:, :, :], tiles_of(YA[1], s).bitcast(F32), 1.0, None, ALU.mult)\
                   .then_inc(staged, 1)

            dve.wait_ge(u2_copied, 1)
            for t in range(TILES):
                if t % (2 * R4) == 0:
                    dve.wait_ge(in2_in[t // (2 * R4)], 16)
                if t == TILES // 2:
                    dve.wait_ge(f1_summed, 1)
                ins = dve.tensor_tensor_reduce(products1[:, t % (TILES // 2), :], in2[t // 16][:, t % 16, :], u2B[:, :], 1.0, 0.0,
                                               ALU.mult, ALU.add, f1[:, t:t + 1])
                if t % (TILES // 2) == TILES // 2 - 1:
                    ins.then_inc(f1_summed, 1)
            dve.wait_ge(f1_summed, 2)
            dve.wait_ge(sums_in, 16 * SUMS_DMAS)
            dve.tensor_scalar(f1[:, :], f1[:, :], b23[:, 0:1], None, ALU.add).then_inc(f1_ready, 1)
            dve.wait_ge(f1_ready, 1)
            dve.tensor_scalar(mf1[:, :], f1[:, :], SLOPE - 1.0, None, ALU.mult).then_inc(mf1_ready, 1)
            dve.wait_ge(x_in, 16)

            def row_sum(s, c, r):
                if c == 0 and r == 0 and s:
                    dve.wait_ge(deg_ready, s)
                if r == 0:
                    dve.wait_ge(adj_in[c], 16 * (s + 1))
                ins = dve.tensor_reduce(dpart[:, c, r:r + 1], quarter[c][:, r, :], AX.X, ALU.add)
                if r == R4 - 1:
                    ins.then_inc(summed, 1)

            def split_lo0(k):
                dve.wait_ge(hi_done, k + 1)
                dve.tensor_tensor(lo[:, k % BUFS, :], TP[k % BUFS][:, :], hi[:, k % BUFS, :].bitcast(F32),
                                  ALU.subtract).then_inc(lo_done, 1)

            def features0(s, j):
                if j < 2:
                    ln_scale(0, s, j)
                if j == 2:
                    ln_relu(0, s, s)
                if j == 3:
                    ln_lo(0, s)

            def norm0(s, j):
                if j == 0:
                    if s:
                        dve.wait_ge(y_ready, s)
                    dve.tensor_copy(xw[:, :, :], tiles_of(X, s)).then_inc(x_new, 1)
                if j in (1, 2):
                    ln_sums(0, s, j - 1)
                if j == 3:
                    ln_variance(0, s)

            for s in range(BLOCKS):
                for c in range(QUARTERS):
                    for i in range(QT):
                        if i < column_blocks_below(s, c):
                            split_lo0(RUN_START[run_of_block(s)] + c * QT + i)
                        if i % 2 and not on_act(s, c):
                            row_sum(s, c, i // 2)
                        if i % 2 and c == 1 and s:
                            features0(s - 1, i // 2)
                        if i % 2 and c == 3:
                            norm0(s, i // 2)
                if s:
                    dve.wait_ge(summed_act, sum(b <= s for b, _ in ACT_QUARTERS))
                dve.wait_ge(summed, sum(b <= s for b, _ in DVE_QUARTERS))
                dve.tensor_reduce(deg[:, s * R4:(s + 1) * R4], dpart[:, :, :].rearrange("p c r -> p r c"), AX.X,
                                  ALU.add).then_inc(deg_ready, 1)
            dve.wait_ge(consts_in, 16 * CONST_DMAS)

            def split_lo(p, s, j):
                dve.wait_ge(hi_done, s * TILES + (p * STEPS + j + 1))
                dve.tensor_tensor(lo[:, j % BUFS, :], TP[j % BUFS][:, :], hi[:, j % BUFS, :].bitcast(F32),
                                  ALU.subtract).then_inc(lo_done, 1)

            def xw_free(prep, s):
                if not (prep == 1 and isinstance(s, int) and s == 0):
                    dve.wait_ge(x_kept, s + (prep - 1) * BLOCKS)

            def take_sums0(o):
                r, b = BELOW + o, ORDER0[o]
                dve.wait_ge(spent, RUN_START[r + 1])
                if b:
                    dve.wait_ge(part_kept, b)
                    ins = dve.tensor_tensor(oT[o % 2][:, :], OT[r % 2][:, :], part_of(b), ALU.add)
                else:
                    ins = dve.tensor_scalar(oT[o % 2][:, :], OT[r % 2][:, :], 1.0, None, ALU.mult)
                ins.then_inc(oT_ready, 1)

            def post0(o, j):
                b = ORDER0[o]
                if j == 0:
                    dve.wait_ge(post_done, o + 1)
                    if o == 0:
                        dve.wait_ge(y_ready, BLOCKS)
                    else:
                        dve.wait_ge(h_ready, o)
                    dve.tensor_tensor(yw[:, :, :], PP[:, 0, :].rearrange("p (r n) -> p r n", r=R4),
                                      per_row(cols_of(d0, b)), ALU.mult).then_inc(scaled, 1)
                if j == 1:
                    dve.wait_ge(scaled, o + 1)
                    dve.tensor_tensor(yw[:, :, :], yw[:, :, :], per_col(b0B[:, :]), ALU.add).then_inc(biased0, 1)
                if j == 2:
                    dve.wait_ge(biased0, o + 1)
                    xw_free(1, o)
                    dve.scalar_tensor_tensor(out=xw[:, :, :], in0=yw[:, :, :], scalar=0.0, in1=tiles_of(X, b),
                                             op0=ALU.max, op1=ALU.add).then_inc(x_new, 1)
                norm_steps(1, o, j - 3, b)

            def norm_steps(prep, s, j, b=None):
                if j in (0, 1):
                    ln_sums(prep, s, j)
                if j == 2:
                    ln_variance(prep, s)
                if j == 3:
                    keep_x(prep, s if b is None else b)
                if j in (5, 6):
                    ln_scale(prep, s, j - 5)
                if j == 7:
                    ln_relu(prep, s, s if b is None else b)
                if j == 8 and prep == 2:
                    ln_lo(prep, s)

            def post2(s, j):
                if j == WEIGH + 2:
                    dve.wait_ge(post_done, s + (BLOCKS + 1))
                    dve.scalar_tensor_tensor(out=yw[:, :, :], in0=PP[:, 0, :].rearrange("p (r n) -> p r n", r=R4),
                                             scalar=0.0, in1=per_row(cols_of(d2, s)), op0=ALU.max, op1=ALU.mult)\
                       .then_inc(scaled, 1)
                if j == WEIGH + 3:
                    dve.wait_ge(scaled, s + (BLOCKS + 1))
                    xw_free(3, s)
                    dve.tensor_tensor(xw[:, :, :], yw[:, :, :], tiles_of(X, s), ALU.add).then_inc(x_new, 1)
                norm_steps(3, s, j - (WEIGH + 4))
                if j in (DOT2, DOT2 + 1):
                    bias_dot(pq, eB, pq_ready, s + 1, j - DOT2)
                if j == DOT2 + 2:
                    dve.wait_ge(sq1_ready, s + 1)
                    dve.tensor_scalar(tiles_of(H, s), pq[:, :, F:2 * F], 1.0, None, ALU.mult).then_inc(q_kept, 1)
                    dve.tensor_scalar(cols_of(nh2, s), sq1[:, :], 1.0, None, ALU.mult).then_inc(nh2_kept, 1)
                mobius(pq[:, :, 0:F], eB, s, s + 1, pq_used, j - MOBIUS2)
                late2(s, j - LATE2)

            def bias_dot(src, bias, ready, n, part):
                if part == 0:
                    dve.wait_ge(ready, n)
                for r in (2 * part, 2 * part + 1):
                    ins = dve.tensor_tensor_reduce(sink2[:, r, :], src[:, r, 0:F], bias[:, :], 1.0, 0.0, ALU.mult,
                                                   ALU.add, dot[:, r:r + 1])
                if part:
                    ins.then_inc(dot_ready, 1)

            def mobius(src, bias, s, n, used, j):
                dst = hv if used is not None else yw
                if j == 0:
                    dve.wait_ge(mix_ready, n)
                    dve.tensor_tensor(dst[:, :, :], src, per_row(al[:, :]), ALU.mult)\
                       .then_inc(used if used is not None else w_scaled, 1)
                if j == 1:
                    dve.tensor_tensor(tw[:, :, :], per_col(bias[:, :]), per_row(be[:, :]), ALU.mult)\
                       .then_inc(bias_scaled, 1)
                if j == 2:
                    dve.wait_ge(bias_scaled, n)
                    dve.tensor_tensor(dst[:, :, :], dst[:, :, :], tw[:, :, :], ALU.add).then_inc(mixed, 1)

            def late2(s, j):
                if j == 0:
                    dve.wait_ge(s_ready, s + 1)
                    dve.tensor_tensor(tw[:, :, :], hv[:, :, :], per_row(sc1[:, :]), ALU.mult).then_inc(y3_scaled, 1)
                if j == 1:
                    dve.wait_ge(y3_scaled, s + 1)
                    dve.tensor_scalar(tiles_of(YB[0], s), tw[:, :, :], 1.0, None, ALU.mult).then_inc(yhi_ready, 1)
                if j == 2:
                    dve.wait_ge(yhi_ready, s + (2 * BLOCKS + 1))
                    dve.tensor_tensor(tiles_of(YB[1], s), tw[:, :, :], tiles_of(YB[0], s).bitcast(F32),
                                      ALU.subtract).then_inc(y_ready, 1)

            def post3(s, j):
                if j == W3:
                    dve.wait_ge(coef_ready, s + 1)
                    dve.tensor_tensor(hv[:, :, :], tiles_of(H, s), per_row(sc0[:, :]), ALU.mult)
                if j == W3 + 1:
                    dve.tensor_tensor(tw[:, :, :], pq[:, :, F:2 * F], per_row(sc1[:, :]), ALU.mult)\
                       .then_inc(pq_used, 1)
                if j == W3 + 2:
                    dve.wait_ge(pq_used, s + (BLOCKS + 1))
                    dve.tensor_tensor(hv[:, :, :], hv[:, :, :], tw[:, :, :], ALU.add).then_inc(w_ready, 1)
                if j in (W3 + 4, W3 + 5):
                    bias_dot(hv, lB, w_ready, s + 1, j - (W3 + 4))
                mobius(hv[:, :, :], lB, s, s + (BLOCKS + 1), None, j - MOBIUS3)
                if j == MOBIUS3 + 3:
                    dve.wait_ge(mixed, s + (BLOCKS + 1))
                    dve.tensor_tensor(tiles_of(X, s), yw[:, :, :], tiles_of(X, s), ALU.add).then_inc(x_final, 1)

            def gcn_pass(p):
                post = (None, post2, post3)[p]

                def body(q, first):
                    for k in range(2 * TILES):
                        e, j = divmod(k, TILES)
                        split_lo(p, q * 2 + e, j)
                        if p == 1 and j == STAGE:
                            stage(p, q * 2 + e)
                        if not first:
                            post(q * 2 + (e - 2), TILES + j)
                        if not (first and e == 0):
                            post(q * 2 + (e - 1), j)
                        elif p == 1:
                            take_attention(BLOCKS - 1, 1, j - 4)
                        elif p == 2:
                            post2(BLOCKS - 2, TILES + j)
                            post2(BLOCKS - 1, j)
                        if p == 2 and first and k == TILES - 1:
                            for late in range(TILES, 2 * TILES):
                                post2(BLOCKS - 1, late)

                blocks_loop(dve, body)
                if p == 2:
                    for j in range(2 * TILES):
                        if j < TILES:
                            post3(BLOCKS - 2, TILES + j)
                        post3(BLOCKS - 1, j)

            for m in range(STEPS - RUN_START[BELOW]):
                split_lo0(RUN_START[BELOW] + m)
                if m == 0:
                    for j in range(4):
                        features0(BLOCKS - 1, j)
                    dve.wait_ge(d_ready, 2)
                for o in range(BLOCKS):
                    if m == RUN_START[BELOW + o + 1] - RUN_START[BELOW] + LAG:
                        take_sums0(o)
                    if 0 <= m - POST0[o] < POST0_STEPS:
                        post0(o, m - POST0[o])
            take_sums0(BLOCKS - 1)
            for j in range(7):
                post0(BLOCKS - 1, j)

            def logits(t, i, beside):
                a, lg = ring[:, i % 2, :], LG[i % 4]
                dve.wait_ge(adj_in[i % 2], (t - i % 2) * 8 + 16 * (ROWTILE_USES + 1))
                for c in range(2):
                    n = t * 2 + (c + 1)
                    half_of = slice(c * HALF, (c + 1) * HALF)
                    dve.wait_ge(bent_added, n)
                    dve.scalar_tensor_tensor(out=lg[:, half_of], in0=lg[:, half_of], scalar=f1[:, bass.ds(t, 1)],
                                             in1=a[:, half_of], op0=ALU.add, op1=ALU.mult)
                    beside(c * 3)
                    if isinstance(n, int) and n == 1:
                        dve.wait_ge(spent, STEPS)
                    else:
                        dve.wait_ge(masked, n - 1)
                    dve.tensor_scalar(R[:, :], a[:, half_of], 0.0, MASKED, ALU.is_le, ALU.mult).then_inc(biased, 1)
                    beside(c * 3 + 1)
                    settle(dve_carry, biased, n)
                    dve.tensor_tensor_reduce(lg[:, half_of], lg[:, half_of], R[:, :], 1.0,
                                             -3e38 if c == 0 else mx[:, 0:1], ALU.add, ALU.max, mx[:, c:c + 1])\
                       .then_inc(masked, 1)
                    if c == 0:
                        beside(2)
                dve.wait_ge(masked, t * 2 + 2)
                dve.tensor_scalar(negm[:, i % 4:i % 4 + 1], mx[:, 1:2], -1.0, None, ALU.mult).then_inc(m_ready, 1)
                beside(5)

            BESIDE = (((), (), (0,), (1,), (2,), (3, 4)), ((5,), (), (7,), (8,), (9,), (10,)))

            def take_attention(s, e, j):
                if j == 0:
                    dve.wait_ge(et_used, (s * R4 + R4) * GROUPS)
                    dve.tensor_tensor(rcp[:, :], rsum[:, e, 0, :], rsum[:, e, 1, :], ALU.add).then_inc(rsum_added, 1)
                    dve.wait_ge(rsum_added, s + 1)
                    dve.reciprocal(rcp[:, :], rcp[:, :]).then_inc(rcp_ready, 1)
                    dve.wait_ge(rcp_ready, s + 1)
                    dve.tensor_tensor(yw[:, :, :], OT[e][:, :].rearrange("p (r n) -> p r n", r=R4),
                                      per_row(rcp[:, :]), ALU.mult).then_inc(l1_taken, 1)
                if j == 1:
                    dve.wait_ge(l1_taken, s + 1)
                    xw_free(2, s)
                    dve.tensor_tensor(xw[:, :, :], yw[:, :, :], tiles_of(X, s), ALU.add).then_inc(x_new, 1)
                norm_steps(2, s, j - 2)

            def attend(q, first):
                for i in range(2 * R4):
                    t = q * 8 + i

                    def beside(n):
                        if not first and i in (2, 3):
                            for j in BESIDE[i - 2][n]:
                                take_attention(q * 2 - 1, 1, j)
                        if i in (6, 7):
                            for j in BESIDE[i - 6][n]:
                                take_attention(q * 2, 0, j)
                        if first and i == 0 and n == 5:
                            for j in range(7, POST0_STEPS):
                                post0(BLOCKS - 1, j)

                    logits(t, i, beside)

            blocks_loop(dve, attend)

            gcn_pass(1)
            gcn_pass(2)

        @block.gpsimd
        def _(pool):
            pool_spare = spare_column(2)

            def idle():
                return pool.tensor_tensor(next(pool_spare), half[:, 0:1], half[:, 0:1], ALU.add)

            pool_carry = (pool, idle)
            pool.memset(idf[:, :], 0.0).then_inc(ident, 1)
            pool.memset(ones[:, :], 1.0).then_inc(consts, 1)
            pool.memset(nhalf[:, :], -0.5).then_inc(consts, 1)
            pool.memset(half[:, :], 0.5).then_inc(consts, 1)
            pool.memset(mone[:, :], -1.0).then_inc(consts, 1)
            pool.memset(one[:, :], 1.0).then_inc(consts, 1)
            pool.wait_ge(ident, 1)
            pool.affine_select(out=idf[:, :], in_=idf[:, :], compare_op=ALU.not_equal, fill=1.0, base=0,
                               pattern=[[-1, P]], channel_multiplier=1).then_inc(ident, 1)
            pool.wait_ge(ident, 2)
            pool.wait_ge(consts, 5)
            pool.tensor_copy(IL[:, 0:F], idf[:, :]).then_inc(il_ready, 1)

            def root(prep, s):
                n = s + (prep * BLOCKS + 1)
                pool.wait_ge(var_ready, n)
                if prep != 2:
                    pool.tensor_tensor(rs[:, :], ve[:, :], nhalf[:, 0:R4], ALU.pow).then_inc(rstd_ready, 1)
                else:
                    pool.tensor_tensor(ps[:, 0, :], ve[:, :], nhalf[:, 0:R4], ALU.pow).then_inc(pow_done, 1)
                    settle(pool_carry, pow_done, s + 1)
                    pool.tensor_tensor(rs[:, :], ps[:, 0, :], cols_of(d2, s), ALU.mult).then_inc(rstd_ready, 1)

            with pool.Fori(0, BLOCKS) as s:
                pool.wait_ge(var_ready, s + 1)
                pool.tensor_tensor(ps[:, 0, :], ve[:, :], nhalf[:, 0:R4], ALU.pow)
                settle(pool_carry, deg_ready, s + 1)
                pool.tensor_tensor(ps[:, 1, :], cols_of(deg, s), one[:, :], ALU.add).then_inc(d_step, 1)
                settle(pool_carry, d_step, s * 2 + 1)
                pool.tensor_tensor(cols_of(d0, s), ps[:, 1, :], nhalf[:, 0:R4], ALU.pow).then_inc(d_step, 1)
                settle(pool_carry, d_step, s * 2 + 2)
                pool.tensor_tensor(rs[:, :], ps[:, 0, :], cols_of(d0, s), ALU.mult).then_inc(rstd_ready, 1)
            pool.tensor_scalar(deg[:, :], deg[:, :], 1.0, None, ALU.add).then_inc(d_ready, 1)
            pool.wait_ge(d_ready, 1)
            pool.tensor_scalar(deg2[:, :], deg[:, :], DEG_EPS, None, ALU.add).then_inc(d_step, 1)
            pool.wait_ge(d_step, 2 * BLOCKS + 1)
            pool.tensor_tensor(d2[:, :], deg2[:, :], nhalf[:, :], ALU.pow).then_inc(d_ready, 1)
            pool.wait_ge(d_ready, 2)

            def add_f2(t, i):
                for c in range(2):
                    half_of = slice(c * HALF, (c + 1) * HALF)
                    pool.wait_ge(bent, t * 2 + (c + 1))
                    pool.tensor_tensor(LG[i % 4][:, half_of], LG[i % 4][:, half_of], f2B[:, half_of], ALU.add)\
                        .then_inc(bent_added, 1)

            add_f2(0, 0)
            with pool.Fori(0, BLOCKS) as s:
                root(1, s)
            for t in range(1, 2 * R4):
                add_f2(t, t)
            root(2, 0)
            with pool.Fori(1, BLOCKS - 1) as s:
                for i in range(R4, 2 * R4):
                    add_f2(s * R4 + i, i)
                root(2, s)
            root(2, BLOCKS - 1)

            class Chain:

                def __init__(self, base):
                    self.base, self.n = base, 0

                def then(self, ins):
                    ins.then_inc(pool_step, 1)
                    self.n += 1
                    pool.wait_ge(pool_step, self.base + self.n)

                def tt(self, out, a, b, op):
                    self.then(pool.tensor_tensor(out, a, b, op))

                def ts(self, out, a, s1, s2, op0, op1=ALU.bypass):
                    idle()
                    self.then(pool.tensor_scalar(out, a, s1, s2, op0, op1) if s2 is not None
                              else pool.tensor_scalar(out, a, s1, None, op0))

            def bounded_norm(ch, out, square, scale=None):
                ch.tt(out, square, half[:, :], ALU.pow)
                if scale is not None:
                    ch.tt(out, out, scale, ALU.mult)
                ch.ts(out, out, H_EPS, None, ALU.max)

            def log_map(ch, out, n_logs):
                ch.ts(nrc[:, :], nrm[:, :], MAX_TANH, None, ALU.min)
                idle().then_inc(nrm_ready, 1)
                t, p, m, c = (ps[:, i, :] for i in range(4))
                ch.tt(t, nrc[:, :], nrc[:, :], ALU.mult)
                ch.ts(p, t, 1.0 / 9, 1.0 / 7, ALU.mult, ALU.add)
                for k in (1.0 / 5, 1.0 / 3, 1.0):
                    ch.tt(p, p, t, ALU.mult)
                    ch.ts(p, p, k, None, ALU.add)
                ch.ts(m, t, 1.0 / 64, None, ALU.is_lt)
                ch.tt(out, nrm[:, :], mone[:, :], ALU.pow)
                ch.ts(c, out, 1.0 / MAX_TANH, None, ALU.max)
                ch.tt(out, out, nrc[:, :], ALU.mult)
                pool.wait_ge(ln_ready, n_logs)
                lg = ps[:, 4, :]
                ch.tt(lg, ln1[:, :], ln2[:, :], ALU.subtract)
                ch.tt(lg, lg, half[:, :], ALU.mult)
                ch.tt(lg, lg, c, ALU.mult)
                ch.tt(p, p, lg, ALU.subtract)
                ch.tt(p, p, m, ALU.mult)
                ch.tt(p, p, lg, ALU.add)
                ch.tt(out, out, p, ALU.mult)

            def mix(ch, square, y2c, scale, n_sq, n_dot, n_tanhs):
                pool.wait_ge(sq2_ready, n_sq)
                pool.wait_ge(dot_ready, n_dot)
                bounded_norm(ch, nth[:, :], square, scale)
                idle().then_inc(nth_ready, 1)
                g, xy, x2, a, d = (ps[:, i, :] for i in range(5))
                ch.tt(g, nth[:, :], mone[:, :], ALU.pow)
                if scale is not None:
                    ch.tt(g, g, scale, ALU.mult)
                pool.wait_ge(th_ready, n_tanhs)
                ch.tt(g, g, th[:, :], ALU.mult)
                ch.tt(xy, g, dot[:, :], ALU.mult)
                ch.tt(x2, g, g, ALU.mult)
                ch.tt(x2, x2, square, ALU.mult)
                ch.ts(xy, xy, 2.0, 1.0, ALU.mult, ALU.add)
                yy = y2c.to_broadcast([P, R4])
                ch.tt(a, xy, yy, ALU.add)
                ch.tt(d, x2, yy, ALU.mult)
                ch.tt(d, d, xy, ALU.add)
                ch.ts(d, d, H_EPS, None, ALU.max)
                ch.tt(d, d, mone[:, :], ALU.pow)
                ch.tt(a, a, g, ALU.mult)
                ch.tt(al[:, :], a, d, ALU.mult)
                ch.ts(x2, x2, -1.0, 1.0, ALU.mult, ALU.add)
                ch.tt(be[:, :], x2, d, ALU.mult)
                idle().then_inc(mix_ready, 1)

            def post2(s):
                root(3, s)
                settle(pool_carry, sq1_ready, s + 1)
                ch = Chain(s * PER2)
                bounded_norm(ch, nrm[:, :], sq1[:, :])
                log_map(ch, sc0[:, :], s * 2 + 1)
                mix(ch, sq2[:, :], y2[:, 0:1], sc0[:, :], s + 1, s + 1, s + 1)
                settle(pool_carry, sq3_ready, s + 1)
                bounded_norm(ch, nrm[:, :], sq3[:, :])
                log_map(ch, sc1[:, :], s * 2 + 2)
                idle().then_inc(s_ready, 1)
                assert ch.n == PER2, ch.n

            def post3(s):
                settle(pool_carry, sq1_ready, s + (BLOCKS + 1))
                ch = Chain(s * PER3 + PER2 * BLOCKS)
                bounded_norm(ch, nth[:, :], sq1[:, :])
                idle().then_inc(nth_ready, 1)
                g, n2 = ps[:, 5, :], ps[:, 6, :]
                ch.tt(g, nth[:, :], mone[:, :], ALU.pow)
                pool.wait_ge(th_ready, s * 2 + (BLOCKS + 1))
                ch.tt(g, g, th[:, :], ALU.mult)
                ch.tt(n2, g, g, ALU.mult)
                ch.tt(n2, n2, sq1[:, :], ALU.mult)
                ch.tt(n2, n2, cols_of(nh2, s), ALU.add)
                bounded_norm(ch, nrm[:, :], n2)
                log_map(ch, sc0[:, :], s + (2 * BLOCKS + 1))
                ch.tt(sc1[:, :], sc0[:, :], g, ALU.mult)
                idle().then_inc(coef_ready, 1)
                mix(ch, sq2[:, :], y2[:, 1:2], None, s + (BLOCKS + 1), s + (BLOCKS + 1), s * 2 + (BLOCKS + 2))
                assert ch.n == PER3, ch.n

            pool.wait_ge(y2_done, 2)
            with pool.Fori(0, BLOCKS) as s:
                post2(s)
            pool.wait_ge(nh2_kept, BLOCKS)
            with pool.Fori(0, BLOCKS) as s:
                post3(s)


_INS = ['x', 'adj', 'L0_gnn_W', 'L0_gnn_b', 'L1_gnn_inlayer2', 'L1_gnn_W1', 'L1_gnn_w2', 'L1_gnn_b2', 'L1_gnn_w3',
        'L1_gnn_b3', 'L2_gnn_weight', 'L3_gnn_embed', 'L3_gnn_layer', 'L3_gnn_embed_bias', 'L3_gnn_layer_bias']


def kernel(**inputs):
    import numpy as _np
    import concourse.bacc as _bacc
    from concourse import mybir as _mybir
    from concourse.bass_utils import run_bass_kernel_spmd as _run

    nc = _bacc.Bacc("TRN2", target_bir_lowering=False, num_devices=1)
    arrays, args = {}, []
    for name in _INS:
        a = _np.ascontiguousarray(inputs[name])
        if a.ndim == 0:
            a = a.reshape(1)
        arrays[f"in_{name}_dram"] = a
        args.append(nc.dram_tensor(f"in_{name}_dram", a.shape, _mybir.dt.from_np(a.dtype), kind="ExternalInput").ap())
    out = nc.dram_tensor("out_0_dram", (4096, 128), _mybir.dt.float32, kind="ExternalOutput").ap()
    build(nc, *args, out)
    r = _run(nc, [arrays], core_ids=[0])
    return r.results[0]["out_0_dram"]
```
